# Optimizing a Trainium2 kernel written in Bass

```python
import numpy as np
import jax
import jax.numpy as jnp

def _softmax(x, axis=-1):
    return jax.nn.softmax(x, axis=axis)

def _gelu(x):
    return jax.nn.gelu(x, approximate=True)

def _silu(x):
    return jax.nn.silu(x)

def _sigmoid(x):
    return jax.nn.sigmoid(x)

def _layernorm(x, axis=-1, eps=1e-05):
    m = jnp.mean(x, axis=axis, keepdims=True)
    v = jnp.var(x, axis=axis, keepdims=True)
    return (x - m) / jnp.sqrt(v + eps)

def _scatter_add(tgt, idx, src, axis=0):
    return tgt.at[idx].add(src)

def _segment_sum(src, seg, n):
    return jax.ops.segment_sum(src, seg, n)
kernel_name = 'mk_xattn_ffn_d2_seqx_r8_48dc53'

def setup_inputs(seed: int=0):
    np.random.seed(seed)
    _w = jnp.asarray

    def _rec_inputs():
        import jax
        import jax.numpy as jnp
        _rk = jax.random.key(seed)
        x = -0.000125 + 0.9999 * jax.random.normal(jax.random.fold_in(_rk, 1), (32, 100, 256), jnp.float32)
        _lenS = 100 - jax.random.randint(jax.random.fold_in(_rk, 7), (32,), 0, max(1, 100 // 4) + 1, jnp.int32)
        _lenS2 = 1444 - jax.random.randint(jax.random.fold_in(_rk, 8), (32,), 0, max(1, 1444 // 4) + 1, jnp.int32)
        _ctx_2048P = jax.random.normal(jax.random.fold_in(_rk, 11), (32, 16, 256), jnp.float32)
        _ctx_2048c = jax.random.dirichlet(jax.random.fold_in(_rk, 511), 0.3 * jnp.ones((16,), jnp.float32), (32, 1444))
        _ctx_2048t = jnp.einsum('bsk,bkd->bsd', _ctx_2048c, _ctx_2048P)
        _ctx_2048t = _ctx_2048t * jax.lax.rsqrt(jnp.mean(jnp.square(_ctx_2048t)) + 1e-12) * 0.953939
        ctx_2048 = 4.13588e-05 + 0.999923 * (_ctx_2048t + 0.3 * jax.random.normal(jax.random.fold_in(_rk, 611), (32, 1444, 256), jnp.float32))
        _validS = jnp.arange(100)[None, :] < _lenS[:, None]
        _validS2 = jnp.arange(1444)[None, :] < _lenS2[:, None]
        _causal = jnp.tril(jnp.ones((100, 100), dtype=bool))
        mask_BxSxS2_ff0 = jnp.where(jnp.ones((32, 100, 1444), dtype=bool), 0.0, -1000000000.0).astype(jnp.float32)
        return (x, ctx_2048, mask_BxSxS2_ff0)
    x, ctx_2048, mask_BxSxS2_ff0 = _rec_inputs()

    def _L0_xattn_setup():
        import jax, jax.numpy as jnp
        import numpy as np
        D_MODEL = 256
        NUM_HEADS = 16
        HEAD_DIM = D_MODEL // NUM_HEADS
        key = jax.random.key(seed)
        ks = jax.random.split(key, 10)
        B, S, T = (4, 512, 128)
        s = 1.0 / np.sqrt(D_MODEL)
        inp = {'query': jax.random.normal(ks[0], (B, S, D_MODEL), jnp.float32), 'key_value': jax.random.normal(ks[1], (B, T, D_MODEL), jnp.float32), 'Wq': jax.random.normal(ks[2], (D_MODEL, D_MODEL), jnp.float32) * s, 'bq': jnp.zeros((D_MODEL,), jnp.float32), 'Wk': jax.random.normal(ks[3], (D_MODEL, D_MODEL), jnp.float32) * s, 'bk': jnp.zeros((D_MODEL,), jnp.float32), 'Wv': jax.random.normal(ks[4], (D_MODEL, D_MODEL), jnp.float32) * s, 'bv': jnp.zeros((D_MODEL,), jnp.float32), 'Wo': jax.random.normal(ks[5], (D_MODEL, D_MODEL), jnp.float32) * s, 'bo': jnp.zeros((D_MODEL,), jnp.float32)}
        return inp
    _L0_xattn_all = _L0_xattn_setup()
    _L0_xattn_in = {k: v for k, v in _L0_xattn_all.items() if k in ('Wq', 'bq', 'Wk', 'bk', 'Wv', 'bv', 'Wo', 'bo')}
    del _L0_xattn_all

    def _L0_ffn_setup():
        import jax, jax.numpy as jnp
        import numpy as np
        HIDDEN = 256
        INTER = 688
        LUT_SIZE = 16

        def _ghost_linear(x, idx, lut):
            w = lut[idx]
            return jnp.einsum('bsh,oh->bso', x, w)
        key = jax.random.key(seed)
        k_x, k_lut, k_g, k_u, k_d = jax.random.split(key, 5)
        x = jax.random.normal(k_x, (2, 512, HIDDEN), dtype=jnp.float32)
        lut = jax.random.normal(k_lut, (LUT_SIZE,), dtype=jnp.float32) * 0.02
        gate_idx = jax.random.randint(k_g, (INTER, HIDDEN), 0, LUT_SIZE, dtype=jnp.int32)
        up_idx = jax.random.randint(k_u, (INTER, HIDDEN), 0, LUT_SIZE, dtype=jnp.int32)
        down_idx = jax.random.randint(k_d, (HIDDEN, INTER), 0, LUT_SIZE, dtype=jnp.int32)
        return {'x': x, 'lut': lut, 'gate_idx': gate_idx, 'up_idx': up_idx, 'down_idx': down_idx}
    _L0_ffn_all = _L0_ffn_setup()
    _L0_ffn_in = {k: v for k, v in _L0_ffn_all.items() if k in ('lut', 'gate_idx', 'up_idx', 'down_idx')}
    del _L0_ffn_all

    def _L1_xattn_setup():
        import jax, jax.numpy as jnp
        import numpy as np
        NUM_HEADS = 16
        EPS = 1e-08

        def _dyn_quant(x):
            s = jnp.maximum(jnp.max(jnp.abs(x), axis=-1, keepdims=True) / 127.0, EPS)
            q = jnp.clip(jnp.round(x / s), -127.0, 127.0)
            return (q, s)

        def _quant_weight(w):
            s = jnp.maximum(jnp.max(jnp.abs(w), axis=1, keepdims=True) / 127.0, EPS)
            q = jnp.clip(jnp.round(w / s), -127.0, 127.0)
            return (q, s)

        def _w8a8_linear(x, w, b):
            qx, sx = _dyn_quant(x)
            qw, sw = _quant_weight(w)
            y = jnp.einsum('bnc,oc->bno', qx, qw) * (sx * sw[:, 0])
            return y + b
        key = jax.random.key(seed)
        ks = jax.random.split(key, 9)
        B, N, L, C = (2, 512, 64, 256)
        sc = 0.02
        return {'x': jax.random.normal(ks[0], (B, N, C), jnp.float32), 'cond': jax.random.normal(ks[1], (B, L, C), jnp.float32), 'mask': jnp.zeros((B, N, L), jnp.float32), 'wq': jax.random.normal(ks[2], (C, C), jnp.float32) * sc, 'bq': jnp.zeros((C,), jnp.float32), 'wk': jax.random.normal(ks[3], (C, C), jnp.float32) * sc, 'bk': jnp.zeros((C,), jnp.float32), 'wv': jax.random.normal(ks[4], (C, C), jnp.float32) * sc, 'bv': jnp.zeros((C,), jnp.float32), 'wo': jax.random.normal(ks[5], (C, C), jnp.float32) * sc, 'bo': jnp.zeros((C,), jnp.float32)}
    _L1_xattn_all = _L1_xattn_setup()
    _L1_xattn_in = {k: v for k, v in _L1_xattn_all.items() if k in ('wq', 'bq', 'wk', 'bk', 'wv', 'bv', 'wo', 'bo')}
    del _L1_xattn_all

    def _L1_ffn_setup():
        import jax, jax.numpy as jnp
        import numpy as np
        E, K = (12, 3)
        B, S, H, I = (2, 256, 256, 640)

        def _forward(x, Wr, br, w1, b1, w2, b2, Wp1, bp1, Wp2, bp2):
            logits = jnp.einsum('bsh,he->bse', x, Wr) + br
            probs = jax.nn.softmax(logits, axis=-1)
            top_vals, top_idx = jax.lax.top_k(probs, K)
            ew = jax.nn.softmax(top_vals, axis=-1)
            out = jnp.zeros_like(x)
            for e in range(E):
                sel = top_idx == e
                mask = sel.any(axis=-1)
                cnt = sel.sum()
                w_e = jnp.sum(jnp.where(sel, ew, 0.0)) / jnp.maximum(cnt, 1).astype(ew.dtype)
                h = jax.nn.relu(jnp.einsum('bsh,hi->bsi', x, w1[e]) + b1[e])
                h = jnp.einsum('bsi,ih->bsh', h, w2[e]) + b2[e]
                out = out + mask[..., None].astype(x.dtype) * (w_e * h)
            pooled = out.mean(axis=1)
            phi = jax.nn.sigmoid(jax.nn.relu(pooled @ Wp1 + bp1) @ Wp2 + bp2)
            phi_mask = (phi > 0.7).astype(out.dtype)[:, :, None]
            return out * (1.0 - phi_mask * 0.8)
        key = jax.random.key(seed)
        ks = jax.random.split(key, 8)
        sH = np.float32(1.0 / np.sqrt(H))
        sI = np.float32(1.0 / np.sqrt(I))
        sH2 = np.float32(1.0 / np.sqrt(H // 2))
        return {'hidden_states': jax.random.normal(ks[0], (B, S, H), jnp.float32), 'Wr': jax.random.normal(ks[1], (H, E), jnp.float32) * sH, 'br': jnp.zeros((E,), jnp.float32), 'w1': jax.random.normal(ks[2], (E, H, I), jnp.float32) * sH, 'b1': jnp.zeros((E, I), jnp.float32), 'w2': jax.random.normal(ks[3], (E, I, H), jnp.float32) * sI, 'b2': jnp.zeros((E, H), jnp.float32), 'Wp1': jax.random.normal(ks[4], (H, H // 2), jnp.float32) * sH, 'bp1': jnp.zeros((H // 2,), jnp.float32), 'Wp2': jax.random.normal(ks[5], (H // 2, 1), jnp.float32) * sH2, 'bp2': jnp.zeros((1,), jnp.float32)}
    _L1_ffn_all = _L1_ffn_setup()
    _L1_ffn_in = {k: v for k, v in _L1_ffn_all.items() if k in ('Wr', 'br', 'w1', 'b1', 'w2', 'b2', 'Wp1', 'bp1', 'Wp2', 'bp2')}
    del _L1_ffn_all
    return {'x': x, 'ctx_2048': ctx_2048, 'mask_BxSxS2_ff0': mask_BxSxS2_ff0, 'L0_xattn_Wq': _L0_xattn_in['Wq'], 'L0_xattn_bq': _L0_xattn_in['bq'], 'L0_xattn_Wk': _L0_xattn_in['Wk'], 'L0_xattn_bk': _L0_xattn_in['bk'], 'L0_xattn_Wv': _L0_xattn_in['Wv'], 'L0_xattn_bv': _L0_xattn_in['bv'], 'L0_xattn_Wo': _L0_xattn_in['Wo'], 'L0_xattn_bo': _L0_xattn_in['bo'], 'L0_ffn_lut': _L0_ffn_in['lut'], 'L0_ffn_gate_idx': _L0_ffn_in['gate_idx'], 'L0_ffn_up_idx': _L0_ffn_in['up_idx'], 'L0_ffn_down_idx': _L0_ffn_in['down_idx'], 'L1_xattn_wq': _L1_xattn_in['wq'], 'L1_xattn_bq': _L1_xattn_in['bq'], 'L1_xattn_wk': _L1_xattn_in['wk'], 'L1_xattn_bk': _L1_xattn_in['bk'], 'L1_xattn_wv': _L1_xattn_in['wv'], 'L1_xattn_bv': _L1_xattn_in['bv'], 'L1_xattn_wo': _L1_xattn_in['wo'], 'L1_xattn_bo': _L1_xattn_in['bo'], 'L1_ffn_Wr': _L1_ffn_in['Wr'], 'L1_ffn_br': _L1_ffn_in['br'], 'L1_ffn_w1': _L1_ffn_in['w1'], 'L1_ffn_b1': _L1_ffn_in['b1'], 'L1_ffn_w2': _L1_ffn_in['w2'], 'L1_ffn_b2': _L1_ffn_in['b2'], 'L1_ffn_Wp1': _L1_ffn_in['Wp1'], 'L1_ffn_bp1': _L1_ffn_in['bp1'], 'L1_ffn_Wp2': _L1_ffn_in['Wp2'], 'L1_ffn_bp2': _L1_ffn_in['bp2']}

def reference(x, ctx_2048, mask_BxSxS2_ff0, L0_xattn_Wq, L0_xattn_bq, L0_xattn_Wk, L0_xattn_bk, L0_xattn_Wv, L0_xattn_bv, L0_xattn_Wo, L0_xattn_bo, L0_ffn_lut, L0_ffn_gate_idx, L0_ffn_up_idx, L0_ffn_down_idx, L1_xattn_wq, L1_xattn_bq, L1_xattn_wk, L1_xattn_bk, L1_xattn_wv, L1_xattn_bv, L1_xattn_wo, L1_xattn_bo, L1_ffn_Wr, L1_ffn_br, L1_ffn_w1, L1_ffn_b1, L1_ffn_w2, L1_ffn_b2, L1_ffn_Wp1, L1_ffn_bp1, L1_ffn_Wp2, L1_ffn_bp2):
    import jax
    import jax.numpy as jnp

    def _L0_xattn_ref(query, key_value, Wq, bq, Wk, bk, Wv, bv, Wo, bo):
        import jax, jax.numpy as jnp
        import numpy as np
        D_MODEL = 256
        NUM_HEADS = 16
        HEAD_DIM = D_MODEL // NUM_HEADS
        B, S, _ = query.shape
        T = key_value.shape[1]
        Q = query @ Wq.T + bq
        K = key_value @ Wk.T + bk
        V = key_value @ Wv.T + bv
        Q = Q.reshape(B, S, NUM_HEADS, HEAD_DIM).transpose(0, 2, 1, 3)
        K = K.reshape(B, T, NUM_HEADS, HEAD_DIM).transpose(0, 2, 1, 3)
        V = V.reshape(B, T, NUM_HEADS, HEAD_DIM).transpose(0, 2, 1, 3)
        scale = 1.0 / np.sqrt(HEAD_DIM).astype(np.float32)
        scores = jnp.einsum('bhsd,bhtd->bhst', Q, K) * scale
        attn = jax.nn.softmax(scores, axis=-1)
        ctx = jnp.einsum('bhst,bhtd->bhsd', attn, V)
        ctx = ctx.transpose(0, 2, 1, 3).reshape(B, S, D_MODEL)
        return ctx @ Wo.T + bo

    def _L0_ffn_ref(x, lut, gate_idx, up_idx, down_idx):
        import jax, jax.numpy as jnp
        import numpy as np
        HIDDEN = 256
        INTER = 688
        LUT_SIZE = 16

        def _ghost_linear(x, idx, lut):
            w = lut[idx]
            return jnp.einsum('bsh,oh->bso', x, w)
        gate = _ghost_linear(x, gate_idx, lut)
        up = _ghost_linear(x, up_idx, lut)
        h = jax.nn.silu(gate) * up
        return _ghost_linear(h, down_idx, lut)

    def _L1_xattn_ref(x, cond, mask, wq, bq, wk, bk, wv, bv, wo, bo):
        import jax, jax.numpy as jnp
        import numpy as np
        NUM_HEADS = 16
        EPS = 1e-08

        def _dyn_quant(x):
            s = jnp.maximum(jnp.max(jnp.abs(x), axis=-1, keepdims=True) / 127.0, EPS)
            q = jnp.clip(jnp.round(x / s), -127.0, 127.0)
            return (q, s)

        def _quant_weight(w):
            s = jnp.maximum(jnp.max(jnp.abs(w), axis=1, keepdims=True) / 127.0, EPS)
            q = jnp.clip(jnp.round(w / s), -127.0, 127.0)
            return (q, s)

        def _w8a8_linear(x, w, b):
            qx, sx = _dyn_quant(x)
            qw, sw = _quant_weight(w)
            y = jnp.einsum('bnc,oc->bno', qx, qw) * (sx * sw[:, 0])
            return y + b
        B, N, C = x.shape
        L = cond.shape[1]
        H = NUM_HEADS
        D = C // H
        inv_sqrt_d = np.float32(1.0 / np.sqrt(D))
        q = _w8a8_linear(x, wq, bq).reshape(B, N, H, D).transpose(0, 2, 1, 3)
        k = (cond @ wk.T + bk).reshape(B, L, H, D).transpose(0, 2, 1, 3)
        v = (cond @ wv.T + bv).reshape(B, L, H, D).transpose(0, 2, 1, 3)
        scores = jnp.einsum('bhnd,bhld->bhnl', q, k) * inv_sqrt_d + mask[:, None]
        attn = jax.nn.softmax(scores, axis=-1)
        o = jnp.einsum('bhnl,bhld->bhnd', attn, v)
        o = o.transpose(0, 2, 1, 3).reshape(B, N, C)
        return _w8a8_linear(o, wo, bo)

    def _L1_ffn_ref(hidden_states, Wr, br, w1, b1, w2, b2, Wp1, bp1, Wp2, bp2):
        import jax, jax.numpy as jnp
        import numpy as np
        E, K = (12, 3)
        B, S, H, I = (2, 256, 256, 640)

        def _forward(x, Wr, br, w1, b1, w2, b2, Wp1, bp1, Wp2, bp2):
            logits = jnp.einsum('bsh,he->bse', x, Wr) + br
            probs = jax.nn.softmax(logits, axis=-1)
            top_vals, top_idx = jax.lax.top_k(probs, K)
            ew = jax.nn.softmax(top_vals, axis=-1)
            out = jnp.zeros_like(x)
            for e in range(E):
                sel = top_idx == e
                mask = sel.any(axis=-1)
                cnt = sel.sum()
                w_e = jnp.sum(jnp.where(sel, ew, 0.0)) / jnp.maximum(cnt, 1).astype(ew.dtype)
                h = jax.nn.relu(jnp.einsum('bsh,hi->bsi', x, w1[e]) + b1[e])
                h = jnp.einsum('bsi,ih->bsh', h, w2[e]) + b2[e]
                out = out + mask[..., None].astype(x.dtype) * (w_e * h)
            pooled = out.mean(axis=1)
            phi = jax.nn.sigmoid(jax.nn.relu(pooled @ Wp1 + bp1) @ Wp2 + bp2)
            phi_mask = (phi > 0.7).astype(out.dtype)[:, :, None]
            return out * (1.0 - phi_mask * 0.8)
        return _forward(hidden_states, Wr, br, w1, b1, w2, b2, Wp1, bp1, Wp2, bp2)
    x = x + _L0_xattn_ref(_layernorm(x, axis=-1), ctx_2048, L0_xattn_Wq, L0_xattn_bq, L0_xattn_Wk, L0_xattn_bk, L0_xattn_Wv, L0_xattn_bv, L0_xattn_Wo, L0_xattn_bo)
    x = x + _L0_ffn_ref(_layernorm(x, axis=-1), L0_ffn_lut, L0_ffn_gate_idx, L0_ffn_up_idx, L0_ffn_down_idx)
    x = x + _L1_xattn_ref(_layernorm(x, axis=-1), ctx_2048, mask_BxSxS2_ff0, L1_xattn_wq, L1_xattn_bq, L1_xattn_wk, L1_xattn_bk, L1_xattn_wv, L1_xattn_bv, L1_xattn_wo, L1_xattn_bo)
    x = x + _L1_ffn_ref(_layernorm(x, axis=-1), L1_ffn_Wr, L1_ffn_br, L1_ffn_w1, L1_ffn_b1, L1_ffn_w2, L1_ffn_b2, L1_ffn_Wp1, L1_ffn_bp1, L1_ffn_Wp2, L1_ffn_bp2)
    return x

_drawn_inputs = setup_inputs


def setup_inputs(seed=0):
    import zlib

    import numpy as np

    out = dict(_drawn_inputs(seed))
    spreads = {'L0_xattn_bq': (0.0, 0.1),
     'L0_xattn_bk': (0.0, 0.8),
     'L0_xattn_bv': (0.0, 0.1),
     'L0_xattn_bo': (0.0, 0.1),
     'L1_xattn_bq': (0.0, 0.8),
     'L1_xattn_bk': (0.0, 0.8),
     'L1_xattn_bv': (0.0, 0.1),
     'L1_xattn_bo': (0.0, 0.1),
     'L1_ffn_br': (0.0, 0.1),
     'L1_ffn_b1': (0.0, 0.1),
     'L1_ffn_b2': (0.0, 0.1),
     'L1_ffn_bp1': (0.0, 0.1)}
    factors = {'L1_xattn_wq': 5.758, 'L1_xattn_wk': 3.634}
    for name, (base, spread) in spreads.items():
        noise = np.random.default_rng([zlib.crc32(name.encode()), seed]).standard_normal(out[name].shape)
        drawn = base * np.exp(spread * noise) if base else spread * noise
        out[name] = jnp.asarray(drawn.astype(out[name].dtype))
    for name, factor in factors.items():
        out[name] = (out[name] * factor).astype(out[name].dtype)
    return out
```

```python
from contextlib import ExitStack

import numpy as np
import concourse.bass as bass
from concourse import mybir

F32 = mybir.dt.float32
BF16 = mybir.dt.bfloat16
I32 = mybir.dt.int32
ALU = mybir.AluOpType
ACT = mybir.ActivationFunctionType
AX = mybir.AxisListType

B, S, D = 32, 100, 256
T = 1444
KT = -(-T // 128)
TP = KT * 128
LAST = T - (KT - 1) * 128
H, HD = 16, 16
NP = H // 2
INTER, IT = 688, 6
LUT = 16
E, HID, HT = 12, 640, 5
TOPK = 3
EPS_LN, EPS_Q = 1e-5, 1e-8
MAGIC = 1.5 * 2.0 ** 23
G = NP * KT // 2
TERMS = [(k, *p) for k in range(2) for p in ((0, 0), (0, 1), (1, 0))]
SPLITS = {22 + 6 * (i // 2) + 2 * (i % 2): i for i in range(6)}
LAG = 3
VW = 2 * HD + 1
MC = 482
NB1 = B - 1
FIRST = 3

CHUNK = {g: i for i, g in enumerate((0, 3, 5, 8, 10, 13, 16, 19, 22, 25, 28, 31))}
HALF_END = 41
K_IN = 19
M_MAIN = 16
SIDE_UNITS = (28, 36)


def pieces(l, side):
    at = {g: [] for g in range(G)}
    if side:
        for u in range(24):
            at[K_IN + u * (HALF_END - K_IN) // 24].append(u)
        for u in range(24, SIDE_UNITS[l]):
            at[HALF_END + (u - 24) * (G - HALF_END) // max(SIDE_UNITS[l] - 24, 1)].append(u)
    else:
        n = 48 - SIDE_UNITS[l]
        for i in range(n):
            at[i * M_MAIN // n].append(SIDE_UNITS[l] + i)
    return at


FOLD_1, TURN_1 = M_MAIN, 17
FOLD_0, TURN_0 = HALF_END, 42
MASK_AT = (24, 30, 38)
FFN_AT, FFN_DONE = (14, 20, 26), (16, 21, 27)
UNITS = [[pieces(l, side) for side in range(2)] for l in range(2)]


def wait(eng, sem, value):
    if isinstance(value, int) and value <= 0:
        return
    eng.wait_ge(sem, value)


def exists(b):
    return not isinstance(b, int) or 0 <= b < B


def before(layer, b):
    if not isinstance(b, int):
        return (1, b - 2) if layer == 0 else (0, b + 1)
    if layer == 0:
        return (1, b - 2) if b >= 2 else ((0, b - 1) if b == 1 else None)
    return (0, b + 1) if b < NB1 else (1, b - 1)


def count_before(layer, b, per, k):
    p = before(layer, b)
    return (0, 0) if p is None else (p[0], p[1] * per + k + 1)


class Link:

    def __init__(self, eng, sem, per, b):
        self.eng, self.sem, self.per, self.b, self.k = eng, sem, per, b, 0

    def __call__(self, ins):
        self.k += 1
        ins.then_inc(self.sem, 1)
        self.eng.wait_ge(self.sem, self.b * self.per + self.k)

    def end(self):
        assert self.k == self.per, (self.k, self.per)


def build(nc, a, out):
    with ExitStack() as ctx:
        def sem(name):
            return ctx.enter_context(nc.semaphore(name))

        def sems(name):
            return [sem(f"{name}_l{i}") for i in range(2)]

        program(nc, a, out, ctx, sem, sems)


def program(nc, a, out, ctx, sem, sems):
    def sb(stack, name, shape, dt):
        return stack.enter_context(nc.sbuf_tensor(name, shape, dt))

    x2_dram = nc.dram_tensor("x2_dram", (B, S, D), F32, kind="Internal").ap()
    x3_dram = nc.dram_tensor("x3_dram", (B, S, D), F32, kind="Internal").ap()

    ident = sb(ctx, "ident", [128, 128], F32)
    identb = sb(ctx, "identb", [128, 128], BF16)
    half_neg = sb(ctx, "half_neg", [128, 32], F32)
    bank = [ctx.enter_context(nc.psum_tensor(f"bank{i}", [128, 512], F32)) for i in range(8)]

    p1 = ExitStack()
    ctx_t = sb(p1, "ctx_t", [128, 2, TP], F32)
    c_parts = sb(p1, "c_parts", [128, 2, 2, TP], BF16)
    k_parts = sb(p1, "k_parts", [128, 2, 2, TP], BF16)
    khat = [sb(p1, f"khat{i}", [128, NP, TP], BF16) for i in range(2)]
    vhat = [sb(p1, f"vhat{i}", [128, KT, H, VW], BF16) for i in range(2)]
    qhat = [sb(p1, f"qhat{i}", [128, NP, 2, S], BF16) for i in range(2)]
    q_parts = [sb(p1, f"q_parts{i}", [128, 2, 2, S], BF16) for i in range(2)]
    zeros3 = sb(p1, "zeros3", [3, NP, S], BF16)
    probs = sb(p1, "probs", [128, 4, 432], F32)
    rest = sb(p1, "rest", [128, 4, 432], BF16)
    mask_sb = sb(p1, "mask_sb", [S, TP], F32)
    ident2 = sb(p1, "ident2", [S, 2 * S], F32)
    wk = [sb(p1, f"wk{i}", [128, 2, 2, D], BF16) for i in range(2)]
    wv = [sb(p1, f"wv{i}", [128, 2, 2, D], BF16) for i in range(2)]
    mask_chk = sb(p1, "mask_chk", [S, T], F32)
    mask_abs = sb(p1, "mask_abs", [S, 3], F32)
    mask_any = sb(p1, "mask_any", [1, 1], F32)
    mask_flag = sb(p1, "mask_flag", [1, 1], I32)
    ones_col = sb(p1, "ones_col", [128, 1], F32)
    bk = [sb(p1, f"bk{i}", [128, 2], F32) for i in range(2)]
    wq0 = sb(p1, "wq0", [128, 2, D], F32)
    wo0 = sb(p1, "wo0", [128, 2, D], F32)
    wq1 = sb(p1, "wq1", [128, 2, D], BF16)
    wo1 = sb(p1, "wo1", [128, 2, D], BF16)
    bq_r = [sb(p1, f"bq_r{i}", [S, D], F32) for i in range(2)]
    bv_r = [sb(p1, f"bv_r{i}", [S, D], F32) for i in range(2)]
    bo_r = [sb(p1, f"bo_r{i}", [S, D], F32) for i in range(2)]
    sw_r = [sb(p1, f"sw_r{i}", [S, D], F32) for i in range(2)]
    gate_w = sb(p1, "gate_w", [128, 2, IT * 128], F32)
    up_w = sb(p1, "up_w", [128, 2, IT * 128], F32)
    down_w = sb(p1, "down_w", [128, IT, D], F32)
    lut_b = sb(p1, "lut_b", [128, LUT], F32)
    o_raw = [sb(p1, f"o_raw{i}", [S, NP, 2, VW], F32) for i in range(2)]
    mx3 = sb(p1, "mx3", [S, 2, 8, 3], F32)
    mx = sb(p1, "mx", [S, 2, 8], F32)
    m_neg = sb(p1, "m_neg", [S, 8], F32)
    m_r1 = sb(p1, "m_r1", [S, 8], F32)
    m_nat = [sb(p1, f"m_nat{i}", [S, 2, 3, 4], BF16) for i in range(2)]
    m_parts = [sb(p1, f"m_parts{i}", [24, S], BF16) for i in range(2)]
    stats = sb(p1, "stats", [S, 6], F32)
    mv = sb(p1, "mv", [S, 2], F32)
    veps = sb(p1, "veps", [S, 1], F32)
    rstd = sb(p1, "rstd", [S, 1], F32)
    x_q = sb(p1, "x_q", [S, D], F32)
    x_res = sb(p1, "x_res", [S, D], F32)
    x2_in = sb(p1, "x2_in", [S, D], F32)
    x1 = sb(p1, "x1", [S, D], F32)
    x2 = sb(p1, "x2", [S, D], F32)
    x3 = sb(p1, "x3", [S, D], F32)
    rec = sb(p1, "rec", [S, NP, 2], F32)
    o_n = sb(p1, "o_n", [S, D], F32)
    y = sb(p1, "y", [S, D], F32)
    t1 = sb(p1, "t1", [S, D], F32)
    q_nat = sb(p1, "q_nat", [S, D], F32)
    q_int = sb(p1, "q_int", [S, D], BF16)
    amax = sb(p1, "amax", [S, 1], F32)
    s_q = sb(p1, "s_q", [S, 1], F32)
    rs_q = sb(p1, "rs_q", [S, 1], F32)
    yT = sb(p1, "yT", [128, 2, S], F32)
    qT = sb(p1, "qT", [128, 2, S], BF16)
    ex = sb(p1, "ex", [128, 2, S], F32)
    ex1 = sb(p1, "ex1", [128, 2, S], F32)
    hg = sb(p1, "hg", [128, 2, S], F32)
    hbuf = sb(p1, "hbuf", [128, IT, S], F32)
    w_nat, w_t = (k_parts[:, i, :, 0:1024].bitcast(F32).rearrange("p m (k c) -> p m k c", k=2) for i in range(2))
    w_int = k_parts[:, 0, :, 1024:1536].rearrange("p m (k c) -> p m k c", k=2)
    w_amax = sb(p1, "w_amax", [128, 4], F32)
    w_s = sb(p1, "w_s", [128, 4], F32)
    w_rs = sb(p1, "w_rs", [128, 4], F32)
    w_sb = sb(p1, "w_sb", [128, 4, S], F32)
    p1.close()

    p2 = ctx.enter_context(ExitStack())
    X = sb(p2, "X", [S, B, D], F32)
    Y = sb(p2, "Y", [S, B, D], F32)
    acc = sb(p2, "acc", [S, B, D], F32)
    YT = sb(p2, "YT", [128, 2, B * S], F32)
    w1 = [sb(p2, f"w1_{i}", [128, 2, HID], F32) for i in range(2)]
    w2 = [sb(p2, f"w2_{i}", [128, HT, D], F32) for i in range(2)]
    b1 = [sb(p2, f"b1_{i}", [128, HT], F32) for i in range(2)]
    g_e = [sb(p2, f"g_e{i}", [S, B], F32) for i in range(2)]
    hid = [sb(p2, f"hid{i}", [128, HT, 4 * S], F32) for i in range(2)]
    wr = sb(p2, "wr", [128, 2, E], F32)
    br_r = sb(p2, "br_r", [S, E], F32)
    b2_s = sb(p2, "b2_s", [E, D], F32)
    wp1 = sb(p2, "wp1", [128, 2, 128], F32)
    bp1 = sb(p2, "bp1", [128, 1], F32)
    wp2 = sb(p2, "wp2", [128, 1], F32)
    bp2_r = sb(p2, "bp2_r", [S, 1], F32)
    nbp2 = sb(p2, "nbp2", [S, 1], F32)
    ex3 = sb(p2, "ex3", [S, TOPK, B], F32)
    st6 = sb(p2, "st6", [S, B, 6], F32)
    mean = sb(p2, "mean", [S, B], F32)
    var = sb(p2, "var", [S, B], F32)
    dif = sb(p2, "dif", [S, B], F32)
    rst = sb(p2, "rst", [S, B], F32)
    lg = sb(p2, "lg", [S, B, E], F32)
    pr = sb(p2, "pr", [S, B, E], F32)
    eq = sb(p2, "eq", [S, B, E], F32)
    sel = sb(p2, "sel", [S, TOPK, B, E], F32)
    order = sb(p2, "order", [S, E], F32)
    top = sb(p2, "top", [S, TOPK, B], F32)
    ew = sb(p2, "ew", [S, TOPK, B], F32)
    red = sb(p2, "red", [S, B], F32)
    red2 = sb(p2, "red2", [S, B], F32)
    cm = sb(p2, "cm", [S, 2, B, E], F32)
    cms = sb(p2, "cms", [S, 2, E], F32)
    w_e = sb(p2, "w_e", [S, 2, E], F32)
    gt = sb(p2, "gt", [S, E, B], F32)
    gT = sb(p2, "gT", [E, B, S], F32)
    onesS = sb(p2, "onesS", [S, S], F32)
    pooled = sb(p2, "pooled", [128, 2, B], F32)
    hp = sb(p2, "hp", [128, B], F32)
    wp2b = sb(p2, "wp2b", [128, S], F32)
    fac = sb(p2, "fac", [S, B], F32)

    const_ready = sem("const_ready")
    attn_weights = sem("attn_weights")
    lut_done = sem("lut_done")
    wq_int = sem("wq_int")
    wq_tr = sem("wq_tr")
    wq_ready = sem("wq_ready")
    dve_link = sem("dve_link")
    pool_pro = sem("pool_pro")

    ctx_ready = sems("ctx_ready")
    c_hi, c_lo = sems("c_hi"), sems("c_lo")
    w_split = sem("w_split")
    chk_in, chk_abs, flag_mm, flag_ready = (sem(n) for n in ("chk_in", "chk_abs", "flag_mm", "flag_ready"))
    k_hi, k_mm, kv_lo = sems("kv_hi"), sems("kv_mm"), sems("kv_lo")
    khat_ready = sems("khat_ready")
    qhat_ready = sems("qhat_ready")
    m_mm, m_red = sems("max_mm"), sems("max_red")
    m_fold = [sems(f"max_fold{h}") for h in range(2)]
    m_tr = [sems(f"max_tr{h}") for h in range(2)]
    m_split = [sems(f"max_split{h}") for h in range(2)]
    m_rows = [sems(f"max_rows{h}") for h in range(2)]
    m_link = sems("max_link")
    sc_done, exp_done, res_done, pv_done = sems("sc_done"), sems("exp_done"), sems("res_done"), sems("pv_done")
    o_evac = sems("o_evac")
    o_norm = sems("o_norm")
    mask_ready = sem("mask_ready")
    ln_var = {k: sem(f"ln_var_{k}") for k in ("q0", "ffn", "q1")}
    ln_rstd = {k: sem(f"ln_rstd_{k}") for k in ("q0", "ffn", "q1")}
    steps = ("oT", "wo", "y1T", "ffn0", "ffn1", "ffn2", "down", "q1T", "q1", "q1N",
             "o1T", "wo1", "q0T", "q0", "q0N")
    pe = {k: sem(f"pe_{k}") for k in steps}
    cp = {k: sem(f"cp_{k}") for k in steps}
    dv = {k: sem(f"dv_{k}") for k in ("y1", "h0", "h1", "h2", "x1", "x2", "q1i", "q1n", "q1lo", "o1i", "x3", "y0", "q0n", "q0lo")}
    lk = {k: sem(f"link_{k}") for k in ("post0", "post1", "qprep0")}
    x_q_in, x_res_in, x2_in_s, x2_out, x3_out = (sem(n) for n in ("x_q_in", "x_res_in", "x2_in_s", "x2_out", "x3_out"))

    e_in = sem("e_in")
    x_in = sem("x_in")
    w_in = [sem(f"w_in{i}") for i in range(2)]
    tick = sem("tick")
    e = {k: sem(f"e_{k}") for k in (
        "var", "rstd", "y", "yT_mm", "yT", "logits", "exp_in", "exp", "sums_in", "sums",
        "gates", "gT_mm", "gT", "init_mm", "init", "pool_mm", "pool", "hp_mm", "hp", "z_mm", "z_exp",
        "small", "final")}
    h_mm, h_done, y_mm, y_acc = sem("h_mm"), sem("h_done"), sem("y_mm"), sem("y_acc")
    ge_ready = sem("ge_ready")
    out_sem = sem("out_sem")

    sc_bank, mx_bank, o_bank, kv_bank, ch = bank[0:2], bank[2:4], bank[4:6], bank[6], bank[7]
    chb = ch[:, :].bitcast(BF16)

    def rows(ap, n):
        return ap.partition_broadcast(n)

    def group(g):
        return g // (KT // 2), 2 * (g % (KT // 2))

    w_stage = [khat[0][:, i, 0:4 * D].bitcast(F32).rearrange("p (k o) -> p k o", k=2) for i in range(4)]
    idx_g = khat[1][:, 0:2, :].bitcast(I32)
    idx_u = khat[1][:, 2:4, :].bitcast(I32)
    idx_d = khat[1][:, 4:6, :].bitcast(I32)
    term = khat[1][:, 6:8, :].bitcast(F32)

    block = ctx.enter_context(nc.Block())

    @block.sync
    def _(sp):
        def hold(sem, value):
            wait(sp, sem, value)
            if not isinstance(value, int):
                sp.sem_inc(tick, 1)

        n = [0]

        def w(dst, src):
            n[0] += 1
            sp.dma_start(dst, src).then_inc(attn_weights, 16)

        for l in range(2):
            w(w_stage[2 * l], a[f"wkT{l}"].rearrange("(k p) o -> p k o", p=128))
            w(w_stage[2 * l + 1], a[f"wvT{l}"].rearrange("(k p) o -> p k o", p=128))
            w(bk[l][:, :], a[f"bk{l}"])
            w(bq_r[l][:, :], rows(a[f"bq{l}"], S))
            w(bv_r[l][:, :], rows(a[f"bv{l}"], S))
            w(bo_r[l][:, :], rows(a[f"bo{l}"], S))
        w(wq0[:, :, :], a["wqT0"].rearrange("(k p) o -> p k o", p=128))
        w(wo0[:, :, :], a["woT0"].rearrange("(k p) o -> p k o", p=128))
        w(w_nat[:, 0, :, :], a["wq1"].rearrange("(k p) c -> p k c", p=128))
        w(w_nat[:, 1, :, :], a["wo1"].rearrange("(k p) c -> p k c", p=128))
        w(lut_b[:, :], rows(a["lut"], 128))
        w(idx_g[:, :, 0:INTER], a["gateT"].rearrange("(k p) o -> p k o", p=128))
        w(idx_u[:, :, 0:INTER], a["upT"].rearrange("(k p) o -> p k o", p=128))
        dn = idx_d.rearrange("p j c -> p (j c)").rearrange("p (i o) -> p i o", o=D)
        full = INTER // 128
        w(dn[:, 0:full, :], a["downT"][0:full * 128, :].rearrange("(i p) o -> p i o", p=128))
        w(dn[0:INTER - full * 128, full, :], a["downT"][full * 128:INTER, :])
        assert n[0] == N_DMA

        def load_ctx(l, b):
            pl, v = count_before(l, b, 6, 5)
            hold(c_lo[pl], v)
            src = a["ctxT"][b].rearrange("(k p) t -> p k t", p=128)
            sp.dma_start(ctx_t[:, :, 0:T], src).then_inc(ctx_ready[l], 16)
            sp.dma_start(ctx_t[:, :, T:TP], src[:, :, 0:TP - T]).then_inc(ctx_ready[l], 16)

        def load_qhat(l, b):
            hold(dv["q0lo" if l == 0 else "q1lo"], b + 1)
            hold(sc_done[l], b * G)
            if isinstance(b, int) and b == 0:
                sp.wait_ge(const_ready, N_CONST)
            for s in range(2):
                for r, part in enumerate((0, 0, 1)):
                    p = 64 * s + HD * r
                    sp.dma_start(qhat[l][p:p + HD, :, s, :], q_parts[l][:, s, part, :]).then_inc(qhat_ready[l], 16)
                p = 64 * s + 3 * HD
                sp.dma_start(qhat[l][p:p + 3, :, s, :], zeros3[:, :, :]).then_inc(qhat_ready[l], 16)

        def load_khat(l, b):
            for s in range(2):
                hold(kv_lo[l], b * 12 + 3 * s + 3)
                if s == 0:
                    hold(sc_done[l], b * G)
                    if isinstance(b, int) and b == 0:
                        sp.wait_ge(const_ready, N_CONST)
                        sp.wait_ge(lut_done, 1)
                for r, part in enumerate((0, 1, 0)):
                    p = 64 * s + HD * r
                    sp.dma_start(khat[l][p:p + HD, :, :], k_parts[:, s, part, :]).then_inc(khat_ready[l], 16)

        def load_max(l, b, h):
            hold(m_split[h][l], b + 1)
            hold(m_mm[l], b * 48 + 24 * (h + 1))
            for s in range(2):
                p = 64 * s + 3 * HD
                sp.dma_start(qhat[l][p:p + 3, 4 * h:4 * h + 4, s, :],
                             m_parts[h][12 * s:12 * s + 12, :]).then_inc(m_rows[h][l], 16)

        def slot_a(b):
            side, post, prep = b - 1, b - 2, b + 1
            if exists(side):
                load_qhat(1, side)
            if exists(prep):
                load_ctx(0, prep)
                hold(dv["y0"], prep)
                sp.dma_start(x_q[:, :], a["x"][prep]).then_inc(x_q_in, 16)
            if exists(side):
                hold(flag_ready, side + 1)
                flag = sp.value_load(mask_flag[0:1, 0:1], min_val=0, max_val=1)
                hold(sc_done[1], side * G)
                with sp.If(flag > 0):
                    sp.dma_start(mask_sb[:, 0:T], a["mask"][side]).then_inc(mask_ready, 16)
                with sp.Else():
                    sp.sem_inc(mask_ready, 16)
                load_khat(1, side)
            if exists(b):
                hold(dv["x1"], b)
                sp.dma_start(x_res[:, :], a["x"][b]).then_inc(x_res_in, 16)
            if exists(post):
                hold(dv["x3"], post + 1)
                sp.dma_start(x3_dram[post], x3[:, :]).then_inc(x3_out, 16)
            if exists(b):
                load_max(0, b, 1)
            if exists(side):
                load_max(1, side, 0)

        def slot_b(b):
            main, side = b - 1, b + 1
            if exists(side):
                load_qhat(0, side)
            if exists(b):
                load_ctx(1, b)
                hold(chk_abs, 3 * b)
                sp.dma_start(mask_chk[:, :], a["mask"][b]).then_inc(chk_in, 16)
            if exists(b - 1):
                hold(dv["x3"], b - 1)
                hold(x2_out, 16 * b)
                sp.dma_start(x2_in[:, :], x2_dram[b - 1]).then_inc(x2_in_s, 16)
            if exists(side):
                load_khat(0, side)
            if exists(main):
                load_max(1, main, 1)
            if exists(b):
                hold(dv["x2"], b + 1)
                sp.dma_start(x2_dram[b], x2[:, :]).then_inc(x2_out, 16)
            if exists(side):
                load_max(0, side, 0)

        sp.dma_start(x_q[:, :], a["x"][0]).then_inc(x_q_in, 16)
        load_ctx(0, 0)
        slot_b(-1)
        for b in range(FIRST):
            slot_a(b)
            slot_b(b)
        with sp.Fori(FIRST, NB1) as b:
            slot_a(b)
            slot_b(b)
        for b in (NB1, B):
            slot_a(b)
            slot_b(b)
        slot_a(B + 1)

        sp.wait_ge(x3_out, 16 * B)
        sp.dma_start(X[:, :, :], x3_dram.rearrange("b q d -> q b d")).then_inc(x_in, 16)
        for dst, src in ((wr[:, :, :], a["Wr"].rearrange("(k p) e -> p k e", p=128)),
                         (br_r[:, :], rows(a["br"], S)), (b2_s[:, :], a["b2"]),
                         (wp1[:, :, :], a["Wp1"].rearrange("(k p) o -> p k o", p=128)),
                         (bp1[:, :], a["bp1"]), (wp2[:, :], a["Wp2"]), (bp2_r[:, :], rows(a["bp2"], S))):
            sp.dma_start(dst, src).then_inc(e_in, 16)

        def expert(n, p):
            sp.dma_start(w1[p][:, :, :], a["w1"][n].rearrange("(k p) o -> p k o", p=128)).then_inc(w_in[p], 16)
            sp.dma_start(w2[p][:, :, :], a["w2"][n].rearrange("(k p) o -> p k o", p=128)).then_inc(w_in[p], 16)
            sp.dma_start(b1[p][:, :], a["b1"][n]).then_inc(w_in[p], 16)

        for p in range(2):
            expert(p, p)
        with sp.Fori(0, E // 2 - 1) as i:
            for p in range(2):
                hold(y_mm, (2 * i + p + 1) * B)
                expert(2 * i + p + 2, p)
        for c in range(4):
            sp.wait_ge(e["final"], c + 1)
            sp.dma_start(out[8 * c:8 * c + 8].rearrange("b q d -> q b d"), acc[:, 8 * c:8 * c + 8, :]).then_inc(out_sem, 16)
        sp.wait_ge(out_sem, 64)

    @block.tensor
    def _(te):
        te.wait_ge(const_ready, N_CONST)
        te.wait_ge(attn_weights, 16 * N_DMA)
        te.wait_ge(wq_int, 1)
        for m in range(2):
            for c in range(2):
                for k in range(2):
                    te.transpose(chb[:, (m * 2 + c) * D + k * 128:(m * 2 + c) * D + k * 128 + 128],
                                 w_int[:, m, k, c * 128:c * 128 + 128], identb[:, :])
        for m in range(2):
            for k in range(2):
                last = te.matmul(kv_bank[0:S, m * D + k * 128:m * D + k * 128 + 128],
                                 w_sb[:, 2 * m + k, :], ident[:, :], start=True, stop=True)
        last.then_inc(wq_tr, 1)
        te.wait_ge(wq_ready, 2)

        def scores(l, b, g, masked):
            j, t = group(g)
            if g >= 2:
                te.wait_ge(exp_done[l], b * G + g - 1)
            else:
                pl, v = count_before(l, b, G, G - 2 + g)
                wait(te, exp_done[pl], v)
            if g == 0:
                te.wait_ge(qhat_ready[l], 16 * 8 * (b + 1))
                te.wait_ge(khat_ready[l], 16 * 6 * (b + 1))
            if g % (G // 2) == 0:
                te.wait_ge(m_rows[g // (G // 2)][l], 16 * 2 * (b + 1))
            for n in range(2):
                o = sc_bank[g % 2][:, n * 2 * S:(n + 1) * 2 * S]
                if masked:
                    te.matmul(o, mask_sb[:, (t + n) * 128:(t + n + 1) * 128], ident2[:, :], start=True, stop=False)
                last = te.matmul(o, khat[l][:, j, (t + n) * 128:(t + n + 1) * 128],
                                 qhat[l][:, j, :, :].rearrange("p s q -> p (s q)"), start=not masked, stop=True)
            last.then_inc(sc_done[l], 1)

        def values(l, b, g):
            j, t = group(g)
            te.wait_ge(res_done[l], b * G + g + 1)
            if g % (KT // 2) == 0:
                if j >= 2:
                    te.wait_ge(o_evac[l], b * NP + j - 1)
                else:
                    pl, v = count_before(l, b, NP, NP - 2 + j)
                    wait(te, o_evac[pl], v)
            pb = probs[:, g % 4, :].bitcast(BF16)
            for s in range(2):
                o = o_bank[j % 2][:, s * VW:(s + 1) * VW]
                for n in range(2):
                    r = LAST if t + n == KT - 1 else 128
                    c = (2 * n + s) * S
                    v = vhat[l][0:r, t + n, s * NP + j, :]
                    te.matmul(o, pb[0:r, 2 * c + 1:2 * c + 256:2], v, start=(t + n == 0 and s == 0),
                              stop=False, skip_group_check=True)
                    last = te.matmul(o, rest[0:r, g % 4, c:c + 128], v, start=False,
                                     stop=(t + n == KT - 1), skip_group_check=True)
            last.then_inc(pv_done[l], 1)

        def chunk(l, b, i, half):
            if half:
                pass
            elif i == 0:
                te.wait_ge(c_lo[l], 6 * (b + 1))
                pl, v = count_before(l, b, 12, 11)
                wait(te, kv_lo[pl], v)
            else:
                te.wait_ge(kv_lo[l], b * 12 + i)
            if i < 6:
                s, c = i // 3, i % 3
                for n, (k, pw, pc) in list(enumerate(TERMS))[3 * half:3 * half + 3]:
                    last = te.matmul(kv_bank[:, :], wk[l][:, pw, k, s * 128:s * 128 + 128],
                                     c_parts[:, pc, k, c * 512:c * 512 + 512], start=(n == 0), stop=(n == 5))
            else:
                t = 2 * (i - 6) + half
                for n, (k, pw, pc) in enumerate(TERMS):
                    last = te.matmul(kv_bank[:, half * D:(half + 1) * D], c_parts[:, pc, k, t * 128:t * 128 + 128],
                                     wv[l][:, pw, k, :], start=(n == 0), stop=(n == 5))
            if half:
                last.then_inc(k_mm[l], 1)

        def maxima(l, b, u, masked):
            hu, c = u // 3, u % 3
            j, s = hu // 2, hu % 2
            n = min(MC, T - c * MC)
            if u == 0:
                te.wait_ge(qhat_ready[l], 16 * 8 * (b + 1))
                te.wait_ge(khat_ready[l], 16 * 6 * (b + 1))
                if masked:
                    te.wait_ge(mask_ready, 16 * (b + 1))
            if u >= 2:
                te.wait_ge(m_red[l], b * 48 + u - 1)
            else:
                pl, v = count_before(l, b, 48, 46 + u)
                wait(te, m_red[pl], v)
            o = mx_bank[u % 2][0:S, 0:n]
            if masked:
                te.matmul(o, ident[0:S, 0:S], mask_sb[:, c * MC:c * MC + n], start=True, stop=False)
            te.matmul(o, qhat[l][:, j, s, :], khat[l][:, j, c * MC:c * MC + n],
                      start=not masked, stop=True).then_inc(m_mm[l], 1)

        def max_turn(l, b, h):
            te.wait_ge(m_fold[h][l], b + 1)
            te.transpose(chb[0:24, 0:S], m_nat[h][:, :, :, :].rearrange("q s k j -> q (s k j)"),
                         identb[0:S, 0:S]).then_inc(m_tr[h][l], 1)

        def turn(src, key, to=None, idn=None):
            for k in range(2):
                last = te.transpose((to or ch)[:, k * S:(k + 1) * S], src[:, k * 128:k * 128 + 128],
                                    (idn or ident)[0:S, 0:S])
            last.then_inc(pe[key], 1)

        def product(xT, wt, key, n=2):
            for k in range(n):
                last = te.matmul(ch[0:S, 0:D], xT[:, k, :], wt[:, k, :], start=(k == 0), stop=(k == n - 1))
            last.then_inc(pe[key], 1)

        def chain_a(b, g):
            post, prep = b - 2, b + 1
            if exists(post):
                if g == 7:
                    te.wait_ge(dv["o1i"], post + 1)
                    turn(q_int, "o1T", chb, identb)
                if g == 9:
                    te.wait_ge(cp["o1T"], post + 1)
                    product(qT, wo1, "wo1")
            if exists(prep):
                if g == 12:
                    te.wait_ge(dv["y0"], prep + 1)
                    turn(y, "q0T")
                if g == 14:
                    te.wait_ge(cp["q0T"], prep + 1)
                    product(yT, wq0, "q0")
                if g == 19:
                    te.wait_ge(dv["q0n"], prep + 1)
                    if exists(b):
                        te.wait_ge(m_split[1][0], b + 1)
                    turn(q_nat, "q0N")

        def chain_b(b, g):
            if not exists(b):
                return
            if g == 6:
                te.wait_ge(o_norm[0], b + 1)
                turn(o_n, "oT")
            if g == 8:
                te.wait_ge(cp["oT"], b + 1)
                product(yT, wo0, "wo")
            if g == 12:
                te.wait_ge(dv["y1"], b + 1)
                turn(y, "y1T")
            if g in FFN_AT:
                f = FFN_AT.index(g)
                if f == 0:
                    te.wait_ge(cp["y1T"], b + 1)
                    if isinstance(b, int) and b == 0:
                        te.wait_ge(lut_done, 1)
                else:
                    te.wait_ge(dv[f"h{f - 1}"], b + 1)
                if f == 1 and exists(b - 1):
                    te.wait_ge(m_split[1][1], b)
                for n in range(2):
                    for m, wt in enumerate((gate_w, up_w)):
                        for k in range(2):
                            last = te.matmul(ch[:, (2 * n + m) * S:(2 * n + m + 1) * S],
                                             wt[:, k, (2 * f + n) * 128:(2 * f + n + 1) * 128], yT[:, k, :],
                                             start=(k == 0), stop=(k == 1))
                last.then_inc(pe[f"ffn{f}"], 1)
            if g == 29:
                te.wait_ge(dv["h2"], b + 1)
                product(hbuf, down_w, "down", IT)
            if g == 34:
                te.wait_ge(dv["q1i"], b + 1)
                turn(q_int, "q1T", chb, identb)
            if g == 36:
                te.wait_ge(cp["q1T"], b + 1)
                product(qT, wq1, "q1")
            if g == 39:
                te.wait_ge(dv["q1n"], b + 1)
                turn(q_nat, "q1N")
            if g == 45:
                te.wait_ge(chk_abs, 3 * b + 3)
                te.wait_ge(dv["q1lo"], b + 1)
                if exists(b + 1):
                    te.wait_ge(m_split[0][0], b + 2)
                te.matmul(ch[0:1, 0:3], ones_col[0:S, :], mask_abs[:, :], start=True, stop=True).then_inc(flag_mm, 1)

        def slot(prev, main, side, chain, b, masked, bank_read):
            (pl, pb), (ml, mb), (sl, sb_) = prev, main, side
            for g in range(G):
                if exists(mb):
                    scores(ml, mb, g, masked and ml == 1)
                if exists(sb_) and g - 1 in CHUNK:
                    chunk(sl, sb_, CHUNK[g - 1], 1)
                if exists(pb) and g < LAG:
                    values(pl, pb, G - LAG + g)
                if exists(mb) and g >= LAG:
                    values(ml, mb, g - LAG)
                for job, units in ((main, UNITS[ml][0]), (side, UNITS[sl][1])):
                    if exists(job[1]):
                        for u in units[g]:
                            maxima(*job, u, masked and job[0] == 1)
                if exists(mb) and g == TURN_1:
                    key, done = bank_read
                    if exists(done):
                        te.wait_ge(dv[key], done + 1)
                    max_turn(ml, mb, 1)
                if exists(sb_):
                    if g in CHUNK:
                        chunk(sl, sb_, CHUNK[g], 0)
                    if g == TURN_0:
                        max_turn(sl, sb_, 0)
                chain(b, g)

        def slots(b, masked):
            slot((1, b - 2), (0, b), (1, b - 1), chain_a, b, masked, ("q0n", b + 1))
            slot((0, b), (1, b - 1), (0, b + 1), chain_b, b, masked, ("h0", b))

        def iteration(b):
            if not exists(b - 1):
                slots(b, False)
                return
            te.wait_ge(flag_ready, b)
            te.sem_inc(tick, 1)
            flag = te.value_load(mask_flag[0:1, 0:1], min_val=0, max_val=1)
            with te.If(flag > 0):
                slots(b, True)
            with te.Else():
                slots(b, False)

        for b in range(-1, FIRST):
            iteration(b)
        with te.Fori(FIRST, NB1) as b:
            iteration(b)
        for b in (NB1, B, B + 1):
            iteration(b)

        te.wait_ge(e["y"], 1)
        for b in range(B):
            wait(te, e["yT"], b - 3)
            for k in range(2):
                last = te.transpose(bank[b % 4][:, k * S:(k + 1) * S], Y[:, b, k * 128:k * 128 + 128], ident[0:S, 0:S])
            last.then_inc(e["yT_mm"], 1)
        te.wait_ge(e_in, 16 * N_SMALL)
        te.wait_ge(e["yT"], B)
        for b in range(B):
            for k in range(2):
                last = te.matmul(bank[4][0:S, b * E:(b + 1) * E], YT[:, k, b * S:(b + 1) * S], wr[:, k, :],
                                 start=(k == 0), stop=(k == 1))
        last.then_inc(e["logits"], 1)
        te.wait_ge(e["sums_in"], 1)
        te.matmul(bank[5][0:S, 0:2 * E], onesS[:, :], cms[:, :, :].rearrange("p a e -> p (a e)"),
                  start=True, stop=True).then_inc(e["sums"], 1)
        te.wait_ge(e["gates"], 1)
        for b in range(B):
            if b % 4 == 0:
                wait(te, e["gT"], b // 4 - 1)
            last = te.transpose(bank[b // 4 % 2][0:E, (b % 4) * S:(b % 4 + 1) * S], gt[:, :, b], ident[0:S, 0:S])
            if b % 4 == 3:
                last.then_inc(e["gT_mm"], 1)
        for b in range(B):
            if b % 4 == 0:
                te.wait_ge(e["gT"], b // 4 + 1)
            if b % 2 == 0:
                wait(te, e["init"], b // 2 - 1)
            last = te.matmul(bank[6 + b // 2 % 2][0:S, (b % 2) * D:(b % 2 + 1) * D], gT[:, b, :], b2_s[:, :],
                             start=True, stop=True)
            if b % 2 == 1:
                last.then_inc(e["init_mm"], 1)
        te.wait_ge(e["init"], B // 2)

        def hidden(n, p, tb):
            for i in range(HT):
                m = tb * HT + i
                wait(te, h_done, n * 40 + m - 3)
                for k in range(2):
                    last = te.matmul(bank[m % 4][:, 0:4 * S], w1[p][:, k, i * 128:i * 128 + 128],
                                     YT[:, k, tb * 4 * S:(tb + 1) * 4 * S], start=(k == 0), stop=(k == 1))
                last.then_inc(h_mm, 1)

        def back(n, p, tb):
            te.wait_ge(h_done, n * 40 + tb * HT + HT)
            for q in range(4):
                b = tb * 4 + q
                wait(te, y_acc, n * B + b - 3)
                for i in range(HT):
                    last = te.matmul(bank[4 + q][0:S, 0:D], hid[tb % 2][:, i, q * S:(q + 1) * S], w2[p][:, i, :],
                                     start=(i == 0), stop=(i == HT - 1))
                last.then_inc(y_mm, 1)

        def experts(i):
            for p in range(2):
                n = 2 * i + p
                te.wait_ge(w_in[p], 48 * (i + 1))
                for tb in range(8):
                    hidden(n, p, tb)
                    if tb:
                        back(n, p, tb - 1)
                back(n, p, 7)

        experts(0)
        with te.Fori(1, E // 2) as i:
            experts(i)
        te.wait_ge(y_acc, E * B)
        for k in range(2):
            for b in range(B):
                last = te.matmul(bank[0][:, k * B + b:k * B + b + 1], acc[:, b, k * 128:k * 128 + 128],
                                 onesS[:, 0:1], start=True, stop=True)
        last.then_inc(e["pool_mm"], 1)
        te.wait_ge(e["pool"], 1)
        for k in range(2):
            last = te.matmul(bank[1][:, 0:B], wp1[:, k, :], pooled[:, k, :], start=(k == 0), stop=(k == 1))
        last.then_inc(e["hp_mm"], 1)
        te.wait_ge(e["hp"], 1)
        te.wait_ge(e["small"], 1)
        te.matmul(bank[2][0:S, 0:B], wp2b[:, :], hp[:, :], start=True, stop=True).then_inc(e["z_mm"], 1)

    @block.scalar
    def _(ac):
        ac.wait_ge(wq_tr, 1)
        for m, dst in ((0, wq1), (1, wo1)):
            last = nc.scalar.activation(dst[:, :, :].rearrange("p c o -> p (c o)"), chb[:, m * 2 * D:(m + 1) * 2 * D], ACT.Copy)
        last.then_inc(wq_ready, 1)

        def exps(l, b, g):
            ac.wait_ge(sc_done[l], b * G + g + 1)
            if g >= 4:
                ac.wait_ge(pv_done[l], b * G + g - 3)
            else:
                pl, v = count_before(l, b, G, G - 4 + g)
                wait(ac, pv_done[pl], v)
            nc.scalar.activation(probs[:, g % 4, 0:4 * S], sc_bank[g % 2][:, 0:4 * S], ACT.Exp).then_inc(exp_done[l], 1)

        def evac(l, b, j):
            if j == 0:
                wait(ac, o_norm[l], b)
            ac.wait_ge(pv_done[l], b * G + (KT // 2) * (j + 1))
            nc.scalar.activation(o_raw[l][:, j, :, :].rearrange("p s c -> p (s c)"),
                                 o_bank[j % 2][0:S, 0:2 * VW], ACT.Copy).then_inc(o_evac[l], 1)

        def high(l, b, i):
            ac.wait_ge(k_mm[l], b * 12 + i + 1)
            if i < 6:
                s, c = i // 3, i % 3
                if c == 0:
                    pl, v = count_before(l, b, 96, 95)
                    wait(ac, khat_ready[pl], v)
                nc.scalar.activation(k_parts[:, s, 0, c * 512:c * 512 + 512], kv_bank[:, :], ACT.Identity,
                                     bias=bk[l][:, s:s + 1]).then_inc(k_hi[l], 1)
            else:
                t = 2 * (i - 6)
                wait(ac, pv_done[l], b * G)
                nc.scalar.activation(vhat[l][:, t:t + 2, :, 0:HD],
                                     kv_bank[:, :].rearrange("p (n h d) -> p n h d", n=2, h=H),
                                     ACT.Copy).then_inc(k_hi[l], 1)

        def c_high(l, b, i):
            c, k = i // 2, i % 2
            if i == 0:
                ac.wait_ge(ctx_ready[l], 32 * (b + 1))
            if k == 0:
                pl, v = count_before(l, b, 12, 7 + 2 * c)
                wait(ac, k_mm[pl], v)
            nc.scalar.activation(c_parts[:, 0, k, c * 512:c * 512 + 512], ctx_t[:, k, c * 512:c * 512 + 512],
                                 ACT.Copy).then_inc(c_hi[l], 1)

        def copy_T(key, b, dst, src=None):
            ac.wait_ge(pe[key], b + 1)
            nc.scalar.activation(dst[:, :, :].rearrange("p k q -> p (k q)"), (ch if src is None else src)[:, 0:2 * S],
                                 ACT.Copy).then_inc(cp[key], 1)

        def q_high(l, key, b):
            ac.wait_ge(pe[key], b + 1)
            wait(ac, qhat_ready[l], 16 * 8 * b)
            nc.scalar.activation(q_parts[l][:, :, 0, :], ch[:, 0:2 * S].rearrange("p (s q) -> p s q", s=2),
                                 ACT.Copy, scale=1.0 / HD ** 0.5).then_inc(cp[key], 1)

        def chain_a(b, g):
            post, prep = b - 2, b + 1
            if exists(post) and g == 8:
                copy_T("o1T", post, qT, chb)
            if exists(prep):
                if g == 13:
                    copy_T("q0T", prep, yT)
                if g == 20:
                    q_high(0, "q0N", prep)

        def chain_b(b, g):
            if not exists(b):
                return
            if g == 7:
                copy_T("oT", b, yT)
            if g == 13:
                copy_T("y1T", b, yT)
            if g - 1 in FFN_AT:
                f = FFN_AT.index(g - 1)
                ac.wait_ge(pe[f"ffn{f}"], b + 1)
                nc.scalar.activation(ex[:, :, :], ch[:, 0:4 * S].rearrange("p (n m q) -> p n m q", n=2, m=2)[:, :, 0, :],
                                     ACT.Exp, scale=-1.0).then_inc(cp[f"ffn{f}"], 1)
            if g == 35:
                copy_T("q1T", b, qT, chb)
            if g == 40:
                q_high(1, "q1N", b)

        def slot(prev, main, side, chain, b):
            (pl, pb), (ml, mb), (sl, sb_) = prev, main, side
            for g in range(G):
                if exists(mb):
                    exps(ml, mb, g)
                if exists(sb_) and g - 1 in CHUNK:
                    high(sl, sb_, CHUNK[g - 1])
                if exists(pb) and g == LAG:
                    evac(pl, pb, NP - 1)
                if exists(mb) and g >= 9 and (g - 9) % 6 == 0:
                    evac(ml, mb, (g - 9) // 6)
                chain(b, g)
                if exists(mb + 1) and g in SPLITS:
                    c_high(ml, mb + 1, SPLITS[g])

        def slot_a(b):
            slot((1, b - 2), (0, b), (1, b - 1), chain_a, b)

        def slot_b(b):
            slot((0, b), (1, b - 1), (0, b + 1), chain_b, b)

        slot_a(-1)
        slot_b(-1)
        for b in range(FIRST):
            slot_a(b)
            slot_b(b)
        with ac.Fori(FIRST, NB1) as b:
            slot_a(b)
            slot_b(b)
        for b in (NB1, B):
            slot_a(b)
            slot_b(b)
        slot_a(B + 1)

        for b in range(B):
            ac.wait_ge(e["yT_mm"], b + 1)
            nc.scalar.activation(YT[:, :, b * S:(b + 1) * S], bank[b % 4][:, 0:2 * S].rearrange("p (k q) -> p k q", k=2),
                                 ACT.Copy).then_inc(e["yT"], 1)
        ac.wait_ge(e["exp_in"], 1)
        nc.scalar.activation(pr[:, :, :], lg[:, :, :], ACT.Exp).then_inc(e["exp"], 1)
        ac.wait_ge(e["exp_in"], 2)
        nc.scalar.activation(ex3[:, :, :], ew[:, :, :], ACT.Exp).then_inc(e["exp"], 1)
        for c in range(B // 4):
            ac.wait_ge(e["gT_mm"], c + 1)
            nc.scalar.activation(gT[:, 4 * c:4 * c + 4, :].rearrange("e b q -> e (b q)"), bank[c % 2][0:E, 0:4 * S],
                                 ACT.Copy).then_inc(e["gT"], 1)
        for c in range(B // 2):
            ac.wait_ge(e["init_mm"], c + 1)
            nc.scalar.activation(acc[:, 2 * c:2 * c + 2, :].rearrange("q b d -> q (b d)"), bank[6 + c % 2][0:S, :],
                                 ACT.Copy).then_inc(e["init"], 1)

        def experts(i):
            for p in range(2):
                n = 2 * i + p
                ac.wait_ge(w_in[p], 48 * (i + 1))
                for tb in range(8):
                    wait(ac, y_mm, n * B + (tb - 1) * 4)
                    for k in range(HT):
                        m = tb * HT + k
                        ac.wait_ge(h_mm, n * 40 + m + 1)
                        nc.scalar.activation(hid[tb % 2][:, k, :], bank[m % 4][:, 0:4 * S], ACT.Relu,
                                             bias=b1[p][:, k:k + 1]).then_inc(h_done, 1)

        experts(0)
        with ac.Fori(1, E // 2) as i:
            experts(i)
        ac.wait_ge(e["pool_mm"], 1)
        nc.scalar.activation(pooled[:, :, :].rearrange("p k b -> p (k b)"), bank[0][:, 0:2 * B], ACT.Copy,
                             scale=1.0 / S).then_inc(e["pool"], 1)
        ac.wait_ge(e["hp_mm"], 1)
        nc.scalar.activation(hp[:, :], bank[1][:, 0:B], ACT.Relu, bias=bp1[:, 0:1]).then_inc(e["hp"], 1)
        ac.wait_ge(e["z_mm"], 1)
        nc.scalar.activation(fac[:, :], bank[2][0:S, 0:B], ACT.Exp, scale=-1.0, bias=nbp2[:, 0:1]).then_inc(e["z_exp"], 1)

    @block.gpsimd
    def _(po):
        po.memset(ident[:, :], 0.0).then_inc(pool_pro, 1)
        po.memset(identb[:, :], 0.0).then_inc(pool_pro, 1)
        po.wait_ge(pool_pro, 2)
        for m in (ident, identb):
            po.affine_select(out=m[:, :], in_=m[:, :], compare_op=ALU.not_equal, fill=1.0, base=0,
                             pattern=[[-1, 128]], channel_multiplier=1).then_inc(pool_pro, 1)
        po.wait_ge(pool_pro, 4)
        for l in range(2):
            po.memset(vhat[l][:, :, :, VW - 1:VW], 1.0).then_inc(const_ready, 1)
            po.memset(qhat[l][:, :, :, :], 0.0).then_inc(const_ready, 1)
        po.memset(probs[:, :, 4 * S:432], 0.0).then_inc(const_ready, 1)
        po.memset(rest[:, :, 4 * S:432], 0.0).then_inc(const_ready, 1)
        po.memset(mask_sb[:, T:TP], 0.0).then_inc(const_ready, 1)
        po.memset(zeros3[:, :, :], 0.0).then_inc(const_ready, 1)
        po.memset(half_neg[:, :], -0.5).then_inc(const_ready, 1)
        po.wait_ge(w_split, 1)
        po.memset(khat[0][:, :, :], 1.0).then_inc(const_ready, 1)

        def residual(l, b, g):
            po.wait_ge(exp_done[l], b * G + g + 1)
            hi = probs[:, g % 4, :].bitcast(BF16)[:, 1:2 * 4 * S:2]
            po.tensor_tensor(rest[:, g % 4, 0:4 * S], probs[:, g % 4, 0:4 * S], hi, ALU.subtract).then_inc(res_done[l], 1)

        def power(key, b):
            po.wait_ge(ln_var[key], b + 1)
            po.tensor_tensor(rstd[:, :], veps[:, :], half_neg[0:S, 0:1], ALU.pow).then_inc(ln_rstd[key], 1)

        def chain_a(b, g):
            if exists(b + 1) and g == 7:
                power("q0", b + 1)

        def chain_b(b, g):
            if exists(b):
                if g == 10:
                    power("ffn", b)
                if g == 31:
                    power("q1", b)

        def slot(main, chain, b):
            for g in range(G):
                if exists(main[1]):
                    residual(main[0], main[1], g)
                chain(b, g)

        for g in range(G):
            chain_a(-1, g)
        slot((1, -2), chain_b, -1)
        for b in range(FIRST):
            slot((0, b), chain_a, b)
            slot((1, b - 1), chain_b, b)
        with po.Fori(FIRST, NB1) as b:
            slot((0, b), chain_a, b)
            slot((1, b - 1), chain_b, b)
        for b in (NB1, B):
            slot((0, b), chain_a, b)
            slot((1, b - 1), chain_b, b)
        slot((0, B + 1), chain_a, B + 1)
        po.wait_ge(e["var"], 1)
        po.tensor_tensor(rst[:, :], var[:, :], half_neg[0:S, 0:B], ALU.pow).then_inc(e["rstd"], 1)

    @block.vector
    def _(ve):
        k = [0]

        def link(ins):
            k[0] += 1
            ins.then_inc(dve_link, 1)
            ve.wait_ge(dve_link, k[0])

        ve.wait_ge(pool_pro, 4)
        for i in range(2):
            ve.tensor_copy(ident2[:, i * S:(i + 1) * S], ident[0:S, 0:S]).then_inc(const_ready, 1)
        ve.memset(ones_col[:, :], 1.0).then_inc(const_ready, 1)
        ve.wait_ge(attn_weights, 16 * N_DMA)
        for l in range(2):
            for m, dst in enumerate((wk[l], wv[l])):
                link(ve.tensor_copy(dst[:, 0, :, :], w_stage[2 * l + m]))
                last = ve.tensor_tensor(dst[:, 1, :, :], w_stage[2 * l + m], dst[:, 0, :, :], ALU.subtract)
        last.then_inc(w_split, 1)
        link(ve.tensor_reduce(w_amax[:, :].rearrange("p (m k) -> p m k", m=2), w_nat[:, :, :, :], AX.X, ALU.max,
                              apply_absolute_value=True))
        link(ve.tensor_scalar(w_s[:, :], w_amax[:, :], 1.0 / 127.0, EPS_Q, ALU.mult, ALU.max))
        link(ve.reciprocal(w_rs[:, :], w_s[:, :]))
        for r in range(4):
            m, c = r // 2, r % 2
            link(ve.tensor_scalar(w_t[:, m, c, :], w_nat[:, m, c, :], w_rs[:, r:r + 1], MAGIC, ALU.mult, ALU.add))
        wt = w_t.rearrange("p m k c -> p m (k c)")
        link(ve.tensor_scalar(wt, wt, -MAGIC, 127.0, ALU.add, ALU.min))
        link(ve.tensor_scalar(w_int.rearrange("p m k c -> p m (k c)"), wt, -127.0, None, ALU.max))
        ve.tensor_copy(w_sb[:, :, :], w_s[:, :].rearrange("p (r u) -> p r u", u=1).to_broadcast([128, 4, S])).then_inc(wq_int, 1)
        ve.wait_ge(wq_tr, 1)
        for m in range(2):
            last = ve.tensor_copy(sw_r[m][:, :], kv_bank[0:S, m * D:(m + 1) * D])
        last.then_inc(wq_ready, 1)
        link(ve.memset(gate_w[:, :, :], 0.0))
        link(ve.memset(up_w[:, :, :], 0.0))
        link(ve.memset(down_w[:, :, :], 0.0))
        dn = idx_d.rearrange("p j c -> p (j c)").rearrange("p (i o) -> p i o", o=D)
        tm = term.rearrange("p j c -> p (j c)").rearrange("p (i o) -> p i o", o=D)
        full, tail = INTER // 128, INTER % 128
        for idx, tr, dst in ((idx_g[:, :, 0:INTER], term[:, :, 0:INTER], gate_w[:, :, 0:INTER]),
                             (idx_u[:, :, 0:INTER], term[:, :, 0:INTER], up_w[:, :, 0:INTER]),
                             (dn[:, 0:full, :], tm[:, 0:full, :], down_w[:, 0:full, :]),
                             (dn[0:tail, full, :], tm[0:tail, full, :], down_w[0:tail, full, :])):
            for i in range(LUT):
                lv = lut_b[0:idx.shape[0], i:i + 1]
                if i == 0:
                    link(ve.tensor_scalar(dst, idx, float(i), lv, ALU.is_equal, ALU.mult))
                else:
                    link(ve.tensor_scalar(tr, idx, float(i), lv, ALU.is_equal, ALU.mult))
                    link(ve.tensor_tensor(dst, dst, tr, ALU.add))
        ve.memset(khat[1][:, :, :], 1.0).then_inc(lut_done, 1)
        assert k[0] >= 1

        def reduce_unit(l, b, u):
            hu, c = u // 3, u % 3
            j, s = hu // 2, hu % 2
            h, jj = j // 4, j % 4
            ve.wait_ge(m_mm[l], b * 48 + u + 1)
            ve.tensor_reduce(mx3[:, h, s * 4 + jj, c:c + 1], mx_bank[u % 2][0:S, 0:min(MC, T - c * MC)],
                             AX.X, ALU.max).then_inc(m_red[l], 1)

        def fold(l, b, h):
            ln = Link(ve, m_link[l], 10, b)
            ln.k = 5 * h
            ve.wait_ge(m_red[l], b * 48 + 24 * (h + 1))
            part = [m_nat[h][:, :, k, :] for k in range(3)]
            neg, r1 = (t[:, :].rearrange("q (s j) -> q s j", s=2) for t in (m_neg, m_r1))
            ln(ve.tensor_reduce(mx[:, h, :], mx3[:, h, :, :], AX.X, ALU.max))
            ln(ve.tensor_scalar(m_neg[:, :], mx[:, h, :], -1.0, None, ALU.mult))
            ln(ve.tensor_copy(part[0], neg))
            ln(ve.tensor_tensor(r1, neg, part[0], ALU.subtract))
            ln(ve.tensor_copy(part[1], r1))
            assert ln.k == 5 * h + 5
            ve.tensor_tensor(part[2], r1, part[1], ALU.subtract).then_inc(m_fold[h][l], 1)

        def split(l, b, h):
            ve.wait_ge(m_tr[h][l], b + 1)
            prev = before(l, b)
            if prev is not None:
                wait(ve, m_rows[h][prev[0]], 16 * 2 * (prev[1] + 1))
            ve.tensor_copy(m_parts[h][:, :], chb[0:24, 0:S]).then_inc(m_split[h][l], 1)

        def low(l, b, i):
            ve.wait_ge(k_hi[l], b * 12 + i + 1)
            if i < 6:
                s, c = i // 3, i % 3
                ve.scalar_tensor_tensor(k_parts[:, s, 1, c * 512:c * 512 + 512], kv_bank[:, :], bk[l][:, s:s + 1],
                                        k_parts[:, s, 0, c * 512:c * 512 + 512], ALU.add, ALU.subtract).then_inc(kv_lo[l], 1)
            else:
                t = 2 * (i - 6)
                ve.tensor_tensor(vhat[l][:, t:t + 2, :, HD:2 * HD], kv_bank[:, :].rearrange("p (n h d) -> p n h d", n=2, h=H),
                                 vhat[l][:, t:t + 2, :, 0:HD], ALU.subtract).then_inc(kv_lo[l], 1)

        def c_low(l, b, i):
            c, k = i // 2, i % 2
            ve.wait_ge(c_hi[l], 6 * b + i + 1)
            ve.tensor_tensor(c_parts[:, 1, k, c * 512:c * 512 + 512], ctx_t[:, k, c * 512:c * 512 + 512],
                             c_parts[:, 0, k, c * 512:c * 512 + 512], ALU.subtract).then_inc(c_lo[l], 1)

        def normalise(ln, l, b):
            ve.wait_ge(o_evac[l], (b + 1) * NP)
            ln(ve.reciprocal(rec[:, :, :], o_raw[l][:, :, :, 2 * HD]))
            on = o_n[:, :].rearrange("p (s j d) -> p j s d", s=2, j=NP)
            ln(ve.tensor_tensor(on, o_raw[l][:, :, :, 0:HD], o_raw[l][:, :, :, HD:2 * HD], ALU.add))
            ln(ve.tensor_tensor(on, on, rec[:, :, :].rearrange("p j (s u) -> p j s u", u=1).to_broadcast([S, NP, 2, HD]), ALU.mult))
            ve.tensor_tensor(o_n[:, :], o_n[:, :], bv_r[l][:, :], ALU.add).then_inc(o_norm[l], 1)

        def norm_stats(ln, src, key):
            ln(ve.bn_stats(stats[:, :], src[:, :]))
            ve.sem_inc(tick, 1)
            ln(ve.bn_aggr(mv[:, :], stats[:, :]))
            ve.tensor_scalar(veps[:, :], mv[:, 1:2], EPS_LN, None, ALU.add).then_inc(ln_var[key], 1)

        def norm_apply(src, key, b, done):
            ve.wait_ge(ln_rstd[key], b + 1)
            return ve.tensor_scalar(y[:, :], src[:, :], mv[:, 0:1], rstd[:, 0:1], ALU.subtract, ALU.mult)

        def quantise(ln, src, done):
            ln(ve.tensor_reduce(amax[:, :], src[:, :], AX.X, ALU.max, apply_absolute_value=True))
            ln(ve.tensor_scalar(s_q[:, :], amax[:, :], 1.0 / 127.0, EPS_Q, ALU.mult, ALU.max))
            ln(ve.reciprocal(rs_q[:, :], s_q[:, :]))
            ln(ve.tensor_scalar(t1[:, :], src[:, :], rs_q[:, 0:1], MAGIC, ALU.mult, ALU.add))
            ln(ve.tensor_scalar(t1[:, :], t1[:, :], -MAGIC, 127.0, ALU.add, ALU.min))
            ve.tensor_scalar(q_int[:, :], t1[:, :], -127.0, None, ALU.max).then_inc(done, 1)

        def q_low(l, key, b, done):
            ve.wait_ge(cp[key], b + 1)
            ve.scalar_tensor_tensor(q_parts[l][:, :, 1, :], ch[:, 0:2 * S].rearrange("p (s q) -> p s q", s=2),
                                    1.0 / HD ** 0.5, q_parts[l][:, :, 0, :], ALU.mult, ALU.subtract).then_inc(done, 1)

        state = {}

        def chain_a(b, g):
            post, prep = b - 2, b + 1
            if exists(post):
                if g == 4:
                    state["ln"] = Link(ve, lk["post1"], L_POST1, post)
                    normalise(state["ln"], 1, post)
                    ve.wait_ge(o_norm[1], post + 1)
                    quantise(state["ln"], o_n, dv["o1i"])
                if g == 10:
                    ln = state["ln"]
                    ve.wait_ge(pe["wo1"], post + 1)
                    ln(ve.scalar_tensor_tensor(t1[:, :], ch[0:S, 0:D], s_q[:, 0:1], sw_r[1][:, :], ALU.mult, ALU.mult))
                    ln(ve.tensor_tensor(t1[:, :], t1[:, :], bo_r[1][:, :], ALU.add))
                    ve.wait_ge(x2_in_s, 16 * (post + 1))
                    wait(ve, x3_out, 16 * post)
                    ve.tensor_tensor(x3[:, :], x2_in[:, :], t1[:, :], ALU.add).then_inc(dv["x3"], 1)
                    ln.end()
            if exists(prep):
                if g == 6:
                    state["lnq"] = Link(ve, lk["qprep0"], 2, prep)
                    ve.wait_ge(x_q_in, 16 * (prep + 1))
                    norm_stats(state["lnq"], x_q, "q0")
                    state["lnq"].end()
                if g == 11:
                    norm_apply(x_q, "q0", prep, None).then_inc(dv["y0"], 1)
                if g == 15:
                    ve.wait_ge(pe["q0"], prep + 1)
                    ve.tensor_tensor(q_nat[:, :], ch[0:S, 0:D], bq_r[0][:, :], ALU.add).then_inc(dv["q0n"], 1)
                if g == 21:
                    q_low(0, "q0N", prep, dv["q0lo"])

        def chain_b(b, g):
            if not exists(b):
                return
            if g == 4:
                state["ln"] = Link(ve, lk["post0"], L_POST0, b)
                normalise(state["ln"], 0, b)
            if g == 9:
                ln = state["ln"]
                ve.wait_ge(pe["wo"], b + 1)
                ve.wait_ge(x_res_in, 16 * (b + 1))
                ln(ve.tensor_tensor(t1[:, :], ch[0:S, 0:D], bo_r[0][:, :], ALU.add))
                ve.tensor_tensor(x1[:, :], x_res[:, :], t1[:, :], ALU.add).then_inc(dv["x1"], 1)
                ve.wait_ge(dv["x1"], b + 1)
                norm_stats(ln, x1, "ffn")
            if g == 11:
                norm_apply(x1, "ffn", b, None).then_inc(dv["y1"], 1)
            if g in FFN_DONE:
                f, ln = FFN_DONE.index(g), state["ln"]
                gu = ch[:, 0:4 * S].rearrange("p (n m q) -> p n m q", n=2, m=2)
                ve.wait_ge(cp[f"ffn{f}"], b + 1)
                ln(ve.tensor_scalar(ex1[:, :, :], ex[:, :, :], 1.0, None, ALU.add))
                ln(ve.reciprocal(ex1[:, :, :], ex1[:, :, :]))
                ln(ve.tensor_tensor(hg[:, :, :], gu[:, :, 0, :], ex1[:, :, :], ALU.mult))
                ve.tensor_tensor(hbuf[:, 2 * f:2 * f + 2, :], hg[:, :, :], gu[:, :, 1, :], ALU.mult).then_inc(dv[f"h{f}"], 1)
            if g == 30:
                ln = state["ln"]
                ve.wait_ge(pe["down"], b + 1)
                wait(ve, x2_out, 16 * b)
                ve.tensor_tensor(x2[:, :], x1[:, :], ch[0:S, 0:D], ALU.add).then_inc(dv["x2"], 1)
                ve.wait_ge(dv["x2"], b + 1)
                norm_stats(ln, x2, "q1")
            if g == 32:
                ln = state["ln"]
                ln(norm_apply(x2, "q1", b, None))
                quantise(ln, y, dv["q1i"])
            if g == 37:
                ln = state["ln"]
                ve.wait_ge(pe["q1"], b + 1)
                ln(ve.scalar_tensor_tensor(t1[:, :], ch[0:S, 0:D], s_q[:, 0:1], sw_r[0][:, :], ALU.mult, ALU.mult))
                ve.tensor_tensor(q_nat[:, :], t1[:, :], bq_r[1][:, :], ALU.add).then_inc(dv["q1n"], 1)
            if g in MASK_AT:
                c = MASK_AT.index(g)
                ve.wait_ge(chk_in, 16 * (b + 1))
                ve.tensor_reduce(mask_abs[:, c:c + 1], mask_chk[:, c * MC:min((c + 1) * MC, T)], AX.X, ALU.max,
                                 apply_absolute_value=True).then_inc(chk_abs, 1)
            if g == 46:
                ve.wait_ge(flag_mm, b + 1)
                ln = state["ln"]
                ln(ve.tensor_reduce(mask_any[:, :], ch[0:1, 0:3], AX.X, ALU.max))
                ve.tensor_scalar(mask_flag[:, :], mask_any[:, :], 0.0, None, ALU.is_gt).then_inc(flag_ready, 1)
                ln.end()
            if g == 40:
                q_low(1, "q1N", b, dv["q1lo"])

        L_POST0, L_POST1 = 25, 10

        def slot(main, side, chain, b):
            (ml, mb), (sl, sb_) = main, side
            for g in range(G):
                if exists(sb_) and g - 2 in CHUNK:
                    low(sl, sb_, CHUNK[g - 2])
                for job, units in ((main, UNITS[ml][0]), (side, UNITS[sl][1])):
                    if exists(job[1]):
                        for u in units[g]:
                            reduce_unit(*job, u)
                if exists(mb):
                    if g == FOLD_1:
                        fold(ml, mb, 1)
                    if g == TURN_1 + 1:
                        split(ml, mb, 1)
                if exists(sb_):
                    if g == FOLD_0:
                        fold(sl, sb_, 0)
                    if g == TURN_0 + 1:
                        split(sl, sb_, 0)
                chain(b, g)
                if exists(mb + 1) and g - 1 in SPLITS:
                    c_low(ml, mb + 1, SPLITS[g - 1])

        def slot_a(b):
            slot((0, b), (1, b - 1), chain_a, b)

        def slot_b(b):
            slot((1, b - 1), (0, b + 1), chain_b, b)

        slot_a(-1)
        slot_b(-1)
        for b in range(FIRST):
            slot_a(b)
            slot_b(b)
        with ve.Fori(FIRST, NB1) as b:
            slot_a(b)
            slot_b(b)
        for b in (NB1, B):
            slot_a(b)
            slot_b(b)
        slot_a(B + 1)

        def over_last(ap, n):
            names = "abc"[:len(ap.shape) - 1]
            left = " ".join(names)
            return ap.rearrange(f"p {left[:-1]}({left[-1]} u) -> p {left} u", u=1).to_broadcast([*ap.shape, n])

        def over_batches(ap):
            return ap.rearrange("p (u e) -> p u e", u=1).to_broadcast([S, B, E])

        ve.wait_ge(x_in, 16)
        with ve.Fori(0, B) as b:
            ve.bn_stats(st6[:, b, :], X[:, b, :]).then_inc(dve_link, 1)
        k[0] += B
        ve.wait_ge(dve_link, k[0])
        m0, m1 = st6[:, :, 1], st6[:, :, 4]
        link(ve.tensor_tensor(mean[:, :], m0, m1, ALU.add))
        link(ve.tensor_scalar(mean[:, :], mean[:, :], 0.5, None, ALU.mult))
        link(ve.tensor_tensor(dif[:, :], m0, m1, ALU.subtract))
        link(ve.scalar_tensor_tensor(dif[:, :], dif[:, :], 0.25, dif[:, :], ALU.mult, ALU.mult))
        link(ve.tensor_tensor(var[:, :], st6[:, :, 2], st6[:, :, 5], ALU.add))
        link(ve.scalar_tensor_tensor(var[:, :], var[:, :], 1.0 / D, dif[:, :], ALU.mult, ALU.add))
        ve.tensor_scalar(var[:, :], var[:, :], EPS_LN, None, ALU.add).then_inc(e["var"], 1)
        link(ve.tensor_tensor(Y[:, :, :], X[:, :, :], over_last(mean[:, :], D), ALU.subtract))
        ve.wait_ge(e["rstd"], 1)
        ve.tensor_tensor(Y[:, :, :], Y[:, :, :], over_last(rst[:, :], D), ALU.mult).then_inc(e["y"], 1)
        link(ve.memset(onesS[:, :], 1.0))
        for i in range(E):
            link(ve.memset(order[:, i:i + 1], float(E - i)))
        ve.wait_ge(e_in, 16 * N_SMALL)
        link(ve.tensor_scalar(nbp2[:, :], bp2_r[:, :], -1.0, None, ALU.mult))
        ve.tensor_copy(wp2b[:, :], wp2[:, 0:1].to_broadcast([128, S])).then_inc(e["small"], 1)
        ve.wait_ge(e["logits"], 1)
        link(ve.tensor_tensor(lg[:, :, :], bank[4][0:S, 0:B * E].rearrange("p (b e) -> p b e", e=E), over_batches(br_r[:, :]), ALU.add))
        link(ve.tensor_reduce(red[:, :], lg[:, :, :], AX.X, ALU.max))
        ve.tensor_tensor(lg[:, :, :], lg[:, :, :], over_last(red[:, :], E), ALU.subtract).then_inc(e["exp_in"], 1)
        ve.wait_ge(e["exp"], 1)
        link(ve.tensor_reduce(red[:, :], pr[:, :, :], AX.X, ALU.add))
        link(ve.reciprocal(red[:, :], red[:, :]))
        link(ve.tensor_tensor(pr[:, :, :], pr[:, :, :], over_last(red[:, :], E), ALU.mult))
        for r in range(TOPK):
            link(ve.tensor_reduce(top[:, r, :], pr[:, :, :], AX.X, ALU.max))
            link(ve.tensor_tensor(eq[:, :, :], pr[:, :, :], over_last(top[:, r, :], E), ALU.is_equal))
            link(ve.tensor_tensor(eq[:, :, :], eq[:, :, :], over_batches(order[:, :]), ALU.mult))
            link(ve.tensor_reduce(red[:, :], eq[:, :, :], AX.X, ALU.max))
            link(ve.tensor_tensor(sel[:, r, :, :], eq[:, :, :], over_last(red[:, :], E), ALU.is_equal))
            link(ve.scalar_tensor_tensor(pr[:, :, :], sel[:, r, :, :], -4.0, pr[:, :, :], ALU.mult, ALU.add))
        ve.tensor_tensor(ew[:, :, :], top[:, :, :], top[:, 0:1, :].to_broadcast([S, TOPK, B]), ALU.subtract).then_inc(e["exp_in"], 1)
        ve.wait_ge(e["exp"], 2)
        link(ve.tensor_reduce(red[:, :], ex3[:, :, :].rearrange("p r b -> p b r"), AX.X, ALU.add))
        link(ve.reciprocal(red[:, :], red[:, :]))
        link(ve.tensor_tensor(ew[:, :, :], ex3[:, :, :], red[:, :].rearrange("p (u b) -> p u b", u=1).to_broadcast([S, TOPK, B]), ALU.mult))
        link(ve.tensor_reduce(cm[:, 1, :, :], sel[:, :, :, :].rearrange("p r b e -> p b e r"), AX.X, ALU.add))
        for r in range(TOPK):
            link(ve.tensor_tensor(sel[:, r, :, :], sel[:, r, :, :], over_last(ew[:, r, :], E), ALU.mult))
        link(ve.tensor_reduce(cm[:, 0, :, :], sel[:, :, :, :].rearrange("p r b e -> p b e r"), AX.X, ALU.add))
        for i in range(2):
            last = ve.tensor_reduce(cms[:, i, :], cm[:, i, :, :].rearrange("p b e -> p e b"), AX.X, ALU.add)
        last.then_inc(e["sums_in"], 1)
        ve.wait_ge(e["sums"], 1)
        link(ve.tensor_scalar(w_e[:, 1, :], bank[5][0:S, E:2 * E], 1.0, None, ALU.max))
        link(ve.reciprocal(w_e[:, 1, :], w_e[:, 1, :]))
        link(ve.tensor_tensor(w_e[:, 0, :], bank[5][0:S, 0:E], w_e[:, 1, :], ALU.mult))
        ve.tensor_tensor(gt[:, :, :], cm[:, 1, :, :].rearrange("p b e -> p e b"), over_last(w_e[:, 0, :], B), ALU.mult).then_inc(e["gates"], 1)
        ve.wait_ge(e["gates"], 1)
        ve.wait_ge(e["init"], B // 2)

        def experts(i):
            for p in range(2):
                n = 2 * i + p
                wait(ve, y_acc, n * B)
                ve.tensor_copy(g_e[p][:, :], gt[:, n, :]).then_inc(ge_ready, 1)
                ve.wait_ge(ge_ready, n + 1)
                for b in range(B):
                    ve.wait_ge(y_mm, n * B + b + 1)
                    ve.scalar_tensor_tensor(acc[:, b, :], bank[4 + b % 4][0:S, 0:D], g_e[p][:, b:b + 1], acc[:, b, :],
                                            ALU.mult, ALU.add).then_inc(y_acc, 1)

        experts(0)
        with ve.Fori(1, E // 2) as i:
            experts(i)
        ve.wait_ge(e["z_exp"], 1)
        link(ve.tensor_scalar(fac[:, :], fac[:, :], 1.0, None, ALU.add))
        link(ve.reciprocal(fac[:, :], fac[:, :]))
        link(ve.tensor_scalar(fac[:, :], fac[:, :], 0.7, -0.8, ALU.is_gt, ALU.mult))
        link(ve.tensor_scalar(fac[:, :], fac[:, :], 1.0, None, ALU.add))
        ve.wait_ge(y_acc, E * B)
        for b in range(B):
            last = ve.scalar_tensor_tensor(acc[:, b, :], acc[:, b, :], fac[:, b:b + 1], X[:, b, :], ALU.mult, ALU.add)
            if b % 8 == 7:
                last.then_inc(e["final"], 1)


N_DMA = 21
N_CONST = 13
N_SMALL = 7


def kernel(**inputs):
    import concourse.bacc as _bacc
    from concourse.bass_utils import run_bass_kernel_spmd as _run

    x = {k: np.asarray(v) for k, v in inputs.items()}

    def heads_last(w):
        return w.reshape(2, NP, HD, *w.shape[1:]).swapaxes(1, 2).reshape(w.shape)

    host = {
        "x": x["x"], "ctxT": x["ctx_2048"].transpose(0, 2, 1), "mask": x["mask_BxSxS2_ff0"],
        "wqT0": heads_last(x["L0_xattn_Wq"]).T, "woT0": x["L0_xattn_Wo"].T,
        "wq1": heads_last(x["L1_xattn_wq"]), "wo1": x["L1_xattn_wo"],
        "wkT0": heads_last(x["L0_xattn_Wk"]).T, "wkT1": heads_last(x["L1_xattn_wk"]).T,
        "wvT0": x["L0_xattn_Wv"].T, "wvT1": x["L1_xattn_wv"].T,
        "bk0": heads_last(x["L0_xattn_bk"]).reshape(2, 128).T, "bk1": heads_last(x["L1_xattn_bk"]).reshape(2, 128).T,
        "bq0": heads_last(x["L0_xattn_bq"]), "bq1": heads_last(x["L1_xattn_bq"]),
        "bv0": x["L0_xattn_bv"], "bv1": x["L1_xattn_bv"], "bo0": x["L0_xattn_bo"], "bo1": x["L1_xattn_bo"],
        "lut": x["L0_ffn_lut"], "gateT": x["L0_ffn_gate_idx"].T, "upT": x["L0_ffn_up_idx"].T,
        "downT": x["L0_ffn_down_idx"].T,
        "Wr": x["L1_ffn_Wr"], "br": x["L1_ffn_br"], "w1": x["L1_ffn_w1"], "w2": x["L1_ffn_w2"],
        "b1": x["L1_ffn_b1"].reshape(E, HT, 128).transpose(0, 2, 1), "b2": x["L1_ffn_b2"],
        "Wp1": x["L1_ffn_Wp1"], "bp1": x["L1_ffn_bp1"].reshape(128, 1), "Wp2": x["L1_ffn_Wp2"], "bp2": x["L1_ffn_bp2"],
    }
    nc = _bacc.Bacc("TRN2", target_bir_lowering=False, num_devices=1)
    nc.disable_value_cache = True
    arrays, args = {}, {}
    for name, v in host.items():
        v = np.ascontiguousarray(v)
        arrays[f"in_{name}"] = v
        args[name] = nc.dram_tensor(f"in_{name}", v.shape, mybir.dt.from_np(v.dtype), kind="ExternalInput").ap()
    out = nc.dram_tensor("out_0", (B, S, D), F32, kind="ExternalOutput").ap()
    build(nc, args, out)
    r = _run(nc, [arrays], core_ids=[0])
    return r.results[0]["out_0"]
```

```python
from contextlib import ExitStack

import numpy as np
import concourse.bass as bass
from concourse import mybir

F32 = mybir.dt.float32
BF16 = mybir.dt.bfloat16
I32 = mybir.dt.int32
ALU = mybir.AluOpType
ACT = mybir.ActivationFunctionType
AX = mybir.AxisListType

B, S, D = 32, 100, 256
T = 1444
KT = -(-T // 128)
TP = KT * 128
LAST = T - (KT - 1) * 128
H, HD = 16, 16
NP = H // 2
INTER, IT = 688, 6
LUT = 16
E, HID, HT = 12, 640, 5
TOPK = 3
LOOKUPS = 4 * LUT
EPS_LN, EPS_Q = 1e-5, 1e-8
MAGIC = 1.5 * 2.0 ** 23
G = NP * KT // 2
TERMS = [(k, *p) for k in range(2) for p in ((0, 0), (0, 1), (1, 0))]
SPLITS = {24 + 6 * (i // 2) + 2 * (i % 2): i for i in range(6)}
LAG = 3
VW = 2 * HD + 1
MC = 482
NB1 = B - 1
LAST_IT = B - 2
FIRST = 3

CHUNK = {g: i for i, g in enumerate(range(0, 36, 3))}
HALF_END = 40
K_IN = 20
M_MAIN = 17
SIDE_UNITS = (28, 36)


def pieces(l, side):
    at = {g: [] for g in range(G)}
    if side:
        for u in range(24):
            at[K_IN + u * (HALF_END - K_IN) // 24].append(u)
        for u in range(24, SIDE_UNITS[l]):
            at[HALF_END + (u - 24) * (G - HALF_END) // max(SIDE_UNITS[l] - 24, 1)].append(u)
    else:
        n = 48 - SIDE_UNITS[l]
        for i in range(n):
            at[i * M_MAIN // n].append(SIDE_UNITS[l] + i)
    return at


FOLD_1, TURN_1 = M_MAIN, 18
FOLD_0, TURN_0 = HALF_END, 41
MASK_AT = (14, 28, 36)
FFN_AT = (20, 22, 24)
UNITS = [[pieces(l, side) for side in range(2)] for l in range(2)]


def wait(eng, sem, value):
    if isinstance(value, int) and value <= 0:
        return
    eng.wait_ge(sem, value)


def exists(b):
    return not isinstance(b, int) or 0 <= b < B


def before(layer, b):
    if not isinstance(b, int):
        return (1, b - 2) if layer == 0 else (0, b + 1)
    if layer == 0:
        return (1, b - 2) if b >= 2 else ((0, b - 1) if b == 1 else None)
    return (0, b + 1) if b < NB1 else (1, b - 1)


def count_before(layer, b, per, k):
    p = before(layer, b)
    return (0, 0) if p is None else (p[0], p[1] * per + k + 1)


class Link:

    def __init__(self, eng, sem, per, b, k=0):
        self.eng, self.sem, self.per, self.b, self.k, self.first = eng, sem, per, b, k, k

    def ready(self):
        if self.k > self.first:
            self.eng.wait_ge(self.sem, self.b * self.per + self.k)

    def __call__(self, step):
        self.ready()
        step().then_inc(self.sem, 1)
        self.k += 1

    def end(self):
        assert self.k == self.per, (self.k, self.per)


def build(nc, a, out):
    with ExitStack() as ctx:
        def sem(name):
            return ctx.enter_context(nc.semaphore(name))

        def sems(name):
            return [sem(f"{name}_l{i}") for i in range(2)]

        program(nc, a, out, ctx, sem, sems)


def program(nc, a, out, ctx, sem, sems):
    def sb(stack, name, shape, dt):
        return stack.enter_context(nc.sbuf_tensor(name, shape, dt))

    x2_dram = nc.dram_tensor("x2_dram", (B, S, D), F32, kind="Internal").ap()
    x3_dram = nc.dram_tensor("x3_dram", (B, S, D), F32, kind="Internal").ap()

    ident = sb(ctx, "ident", [128, 128], F32)
    identb = sb(ctx, "identb", [128, 128], BF16)
    half_neg = sb(ctx, "half_neg", [128, 32], F32)
    bank = [ctx.enter_context(nc.psum_tensor(f"bank{i}", [128, 512], F32)) for i in range(8)]

    p1 = ExitStack()
    ctx_t = sb(p1, "ctx_t", [128, 2, TP], F32)
    c_parts = sb(p1, "c_parts", [128, 2, 2, TP], BF16)
    k_parts = sb(p1, "k_parts", [128, 2, 2, TP], BF16)
    khat = [sb(p1, f"khat{i}", [128, NP, TP], BF16) for i in range(2)]
    vhat = [sb(p1, f"vhat{i}", [128, KT, H, VW], BF16) for i in range(2)]
    qhat = [sb(p1, f"qhat{i}", [128, NP, 2, S], BF16) for i in range(2)]
    q_parts = [sb(p1, f"q_parts{i}", [128, 2, 2, S], BF16) for i in range(2)]
    zeros3 = sb(p1, "zeros3", [3, NP, S], BF16)
    probs = sb(p1, "probs", [128, 4, 432], F32)
    rest = sb(p1, "rest", [128, 4, 432], BF16)
    mask_sb = sb(p1, "mask_sb", [S, TP], F32)
    ident2 = sb(p1, "ident2", [S, 2 * S], F32)
    wk = [sb(p1, f"wk{i}", [128, 2, 2, D], BF16) for i in range(2)]
    wv = [sb(p1, f"wv{i}", [128, 2, 2, D], BF16) for i in range(2)]
    mask_chk = sb(p1, "mask_chk", [S, T], F32)
    mask_abs = sb(p1, "mask_abs", [S, 3], F32)
    mask_any = sb(p1, "mask_any", [1, 1], F32)
    mask_flag = sb(p1, "mask_flag", [1, 1], I32)
    ones_col = sb(p1, "ones_col", [128, 1], F32)
    bk = [sb(p1, f"bk{i}", [128, 2], F32) for i in range(2)]
    wq0 = sb(p1, "wq0", [128, 2, D], F32)
    wo0 = sb(p1, "wo0", [128, 2, D], F32)
    wq1 = sb(p1, "wq1", [128, 2, D], BF16)
    wo1 = sb(p1, "wo1", [128, 2, D], BF16)
    bq_r = [sb(p1, f"bq_r{i}", [S, D], F32) for i in range(2)]
    bv_r = [sb(p1, f"bv_r{i}", [S, D], F32) for i in range(2)]
    bo_r = [sb(p1, f"bo_r{i}", [S, D], F32) for i in range(2)]
    sw_r = [sb(p1, f"sw_r{i}", [S, D], F32) for i in range(2)]
    gate_w = sb(p1, "gate_w", [128, 2, IT * 128], F32)
    up_w = sb(p1, "up_w", [128, 2, IT * 128], F32)
    down_w = sb(p1, "down_w", [128, IT, D], F32)
    lut_b = sb(p1, "lut_b", [128, LUT], F32)
    o_raw = [sb(p1, f"o_raw{i}", [S, NP, 2, VW], F32) for i in range(2)]
    mx3 = sb(p1, "mx3", [S, 2, 8, 3], F32)
    mx = sb(p1, "mx", [S, 2, 8], F32)
    m_neg = sb(p1, "m_neg", [S, 8], F32)
    m_r1 = sb(p1, "m_r1", [S, 8], F32)
    m_nat = [sb(p1, f"m_nat{i}", [S, 2, 3, 4], BF16) for i in range(2)]
    m_parts = [sb(p1, f"m_parts{i}", [24, S], BF16) for i in range(2)]
    stats = sb(p1, "stats", [S, 6], F32)
    mv = sb(p1, "mv", [S, 2], F32)
    veps = sb(p1, "veps", [S, 1], F32)
    rstd = sb(p1, "rstd", [S, 1], F32)
    x_q = sb(p1, "x_q", [S, D], F32)
    x_res = sb(p1, "x_res", [S, D], F32)
    x2_in = sb(p1, "x2_in", [S, D], F32)
    x1 = sb(p1, "x1", [S, D], F32)
    x2 = sb(p1, "x2", [S, D], F32)
    x3 = sb(p1, "x3", [S, D], F32)
    rec = sb(p1, "rec", [S, NP, 2], F32)
    o_n = sb(p1, "o_n", [S, D], F32)
    y = sb(p1, "y", [S, D], F32)
    t1 = sb(p1, "t1", [S, D], F32)
    q_nat = sb(p1, "q_nat", [S, D], F32)
    q_int = sb(p1, "q_int", [S, D], BF16)
    amax = sb(p1, "amax", [S, 1], F32)
    s_q = sb(p1, "s_q", [S, 1], F32)
    rs_q = sb(p1, "rs_q", [S, 1], F32)
    yT = sb(p1, "yT", [128, 2, S], F32)
    qT = sb(p1, "qT", [128, 2, S], BF16)
    ex = [sb(p1, f"ex_{i}", [128, 2, S], F32) for i in range(2)]
    gu = [sb(p1, f"gu{i}", [128, 2, 2, S], F32) for i in range(2)]
    ex1 = sb(p1, "ex1", [128, 2, S], F32)
    hg = sb(p1, "hg", [128, 2, S], F32)
    hbuf = sb(p1, "hbuf", [128, IT, S], F32)
    w_nat, w_t = (k_parts[:, i, :, 0:1024].bitcast(F32).rearrange("p m (k c) -> p m k c", k=2) for i in range(2))
    w_int = k_parts[:, 0, :, 1024:1536].rearrange("p m (k c) -> p m k c", k=2)
    w_amax = sb(p1, "w_amax", [128, 4], F32)
    w_s = sb(p1, "w_s", [128, 4], F32)
    w_rs = sb(p1, "w_rs", [128, 4], F32)
    w_sb = gu[0][:, :, :, :].rearrange("p n m q -> p (n m) q")
    p1.close()

    p2 = ctx.enter_context(ExitStack())
    X = sb(p2, "X", [S, B, D], F32)
    y_mem = sb(p2, "y_mem", [128, B * D], F32)
    Y = y_mem[0:S, :].rearrange("q (b d) -> q b d", b=B)
    y_parts = y_mem[:, 0:2 * B * S].bitcast(BF16).rearrange("p (a k t) -> p a k t", a=2, k=2)
    acc = sb(p2, "acc", [S, B, D], F32)
    YT = sb(p2, "YT", [128, 2, B * S], F32)
    w_stage2 = [sb(p2, f"w_stage2_{i}", [128, 2 * HID], F32) for i in range(2)]
    w_parts = [[sb(p2, f"w_parts{i}_{m}", [128, 2, 2 * HID], BF16) for m in range(2)] for i in range(2)]
    w1p = [w_parts[i][0][:, :, :].rearrange("p a (k h) -> p a k h", k=2) for i in range(2)]
    w2p = [w_parts[i][1][:, :, :].rearrange("p a (k o) -> p a k o", k=HT) for i in range(2)]
    b1 = [sb(p2, f"b1_{i}", [128, HT], F32) for i in range(2)]
    g_e = [sb(p2, f"g_e{i}", [S, B], F32) for i in range(2)]
    hid = [sb(p2, f"hid{i}", [128, HT, 4 * S], F32) for i in range(2)]
    hid_lo = [sb(p2, f"hid_lo{i}", [128, HT, 4 * S], BF16) for i in range(2)]
    wr = sb(p2, "wr", [128, 2, E], F32)
    br_r = sb(p2, "br_r", [S, E], F32)
    b2_s = sb(p2, "b2_s", [E, D], F32)
    wp1 = sb(p2, "wp1", [128, 2, 128], F32)
    bp1 = sb(p2, "bp1", [128, 1], F32)
    wp2 = sb(p2, "wp2", [128, 1], F32)
    bp2_r = sb(p2, "bp2_r", [S, 1], F32)
    nbp2 = sb(p2, "nbp2", [S, 1], F32)
    ex3 = sb(p2, "ex3", [S, TOPK, B], F32)
    st6 = sb(p2, "st6", [S, B, 6], F32)
    mean = sb(p2, "mean", [S, B], F32)
    var = sb(p2, "var", [S, B], F32)
    dif = sb(p2, "dif", [S, B], F32)
    rst = sb(p2, "rst", [S, B], F32)
    lg = sb(p2, "lg", [S, B, E], F32)
    pr = sb(p2, "pr", [S, B, E], F32)
    eq = lg
    sel = sb(p2, "sel", [S, TOPK, B, E], F32)
    order = sb(p2, "order", [S, E], F32)
    top = sb(p2, "top", [S, TOPK, B], F32)
    ew = sb(p2, "ew", [S, TOPK, B], F32)
    red = sb(p2, "red", [S, B], F32)
    cm = sb(p2, "cm", [S, 2, B, E], F32)
    cms = sb(p2, "cms", [S, 2, E], F32)
    w_e = sb(p2, "w_e", [S, 2, E], F32)
    gt = sb(p2, "gt", [S, E, B], F32)
    gT = sb(p2, "gT", [E, B, S], F32)
    onesS = sb(p2, "onesS", [S, S], F32)
    pooled = sb(p2, "pooled", [128, 2, B], F32)
    hp = sb(p2, "hp", [128, B], F32)
    wp2b = sb(p2, "wp2b", [128, S], F32)
    fac = sb(p2, "fac", [S, B], F32)

    const_ready = sem("const_ready")
    attn_weights = sem("attn_weights")
    lut_done = sem("lut_done")
    wq_int = sem("wq_int")
    wq_tr = sem("wq_tr")
    wq_ready = sem("wq_ready")
    dve_link = sem("dve_link")
    pool_pro = sem("pool_pro")

    ctx_ready = sems("ctx_ready")
    c_hi, c_lo = sems("c_hi"), sems("c_lo")
    w_split = sem("w_split")
    chk_in, chk_abs = sem("chk_in"), sem("chk_abs")
    flag_mm, flag_ready = sem("flag_mm"), sem("flag_ready")
    kv_hi, kv_mm, kv_lo = sems("kv_hi"), sems("kv_mm"), sems("kv_lo")
    khat_ready = sems("khat_ready")
    qhat_ready = sems("qhat_ready")
    m_mm, m_red = sems("max_mm"), sems("max_red")
    m_fold = [sems(f"max_fold{h}") for h in range(2)]
    m_tr = [sems(f"max_tr{h}") for h in range(2)]
    m_split = [sems(f"max_split{h}") for h in range(2)]
    m_rows = [sems(f"max_rows{h}") for h in range(2)]
    m_link = sems("max_link")
    sc_done, exp_done = sems("sc_done"), sems("exp_done")
    res_done, pv_done = sems("res_done"), sems("pv_done")
    o_evac = sems("o_evac")
    o_norm = sems("o_norm")
    mask_ready = sem("mask_ready")
    ln_var = {k: sem(f"ln_var_{k}") for k in ("q0", "ffn", "q1")}
    ln_rstd = {k: sem(f"ln_rstd_{k}") for k in ("q0", "ffn", "q1")}
    steps = ("oT", "wo", "y1T", "ffn0", "ffn1", "ffn2", "down", "q1T", "q1", "q1N",
             "o1T", "wo1", "q0T", "q0", "q0N")
    pe = {k: sem(f"pe_{k}") for k in steps}
    cp = {k: sem(f"cp_{k}") for k in steps}
    dv = {k: sem(f"dv_{k}") for k in ("y1", "h0", "h1", "h2", "x1", "x2", "q1i", "q1n", "q1lo", "o1i", "x3", "y0", "q0n", "q0lo")}
    lk = {k: sem(f"link_{k}") for k in ("post0", "post1", "qprep0")}
    x_q_in, x_res_in, x2_in_s, x2_out, x3_out = (sem(n) for n in ("x_q_in", "x_res_in", "x2_in_s", "x2_out", "x3_out"))

    e_in = sem("e_in")
    x_in = sem("x_in")
    w_in = sem("w_in")
    w_hi, w_lo = sem("w_hi"), sem("w_lo")
    y_hi, y_lo = sem("y_hi"), sem("y_lo")
    r_done = sem("r_done")
    tick = sem("tick")
    e = {k: sem(f"e_{k}") for k in (
        "var", "rstd", "y", "yT_mm", "yT", "logits", "exp_in", "exp", "sums_in", "sums",
        "gates", "gT_mm", "gT", "init_mm", "init", "phi_mm", "phi",
        "small", "final")}
    h_mm, h_done = sem("h_mm"), sem("h_done")
    y_mm, y_acc = sem("y_mm"), sem("y_acc")
    ge_ready = sem("ge_ready")
    out_sem = sem("out_sem")

    sc_bank, mx_bank, o_bank, kv_bank, ch = bank[0:2], bank[2:4], bank[4:6], bank[6], bank[7]
    chb = ch[:, :].bitcast(BF16)

    def rows(ap, n):
        return ap.partition_broadcast(n)

    def group(g):
        return g // (KT // 2), 2 * (g % (KT // 2))

    w_stage = [khat[0][:, i, 0:4 * D].bitcast(F32).rearrange("p (k o) -> p k o", k=2) for i in range(4)]
    idx_g = khat[1][:, 0:2, :].bitcast(I32)
    idx_u = khat[1][:, 2:4, :].bitcast(I32)
    idx_d = khat[1][:, 4:6, :].bitcast(I32)
    term = khat[1][:, 6:8, :].bitcast(F32)

    block = ctx.enter_context(nc.Block())

    @block.sync
    def _(sp):
        def hold(sem, value):
            wait(sp, sem, value)
            if not isinstance(value, int):
                sp.sem_inc(tick, 1)

        n = [0]

        def w(dst, src):
            n[0] += 1
            sp.dma_start(dst, src).then_inc(attn_weights, 16)

        for l in range(2):
            w(w_stage[2 * l], a[f"wkT{l}"].rearrange("(k p) o -> p k o", p=128))
            w(w_stage[2 * l + 1], a[f"wvT{l}"].rearrange("(k p) o -> p k o", p=128))
            w(bk[l][:, :], a[f"bk{l}"])
            w(bq_r[l][:, :], rows(a[f"bq{l}"], S))
            w(bv_r[l][:, :], rows(a[f"bv{l}"], S))
            w(bo_r[l][:, :], rows(a[f"bo{l}"], S))
        w(wq0[:, :, :], a["wqT0"].rearrange("(k p) o -> p k o", p=128))
        w(wo0[:, :, :], a["woT0"].rearrange("(k p) o -> p k o", p=128))
        w(w_nat[:, 0, :, :], a["wq1"].rearrange("(k p) c -> p k c", p=128))
        w(w_nat[:, 1, :, :], a["wo1"].rearrange("(k p) c -> p k c", p=128))
        w(lut_b[:, :], rows(a["lut"], 128))
        w(idx_g[:, :, 0:INTER], a["gateT"].rearrange("(k p) o -> p k o", p=128))
        w(idx_u[:, :, 0:INTER], a["upT"].rearrange("(k p) o -> p k o", p=128))
        dn = idx_d.rearrange("p j c -> p (j c)").rearrange("p (i o) -> p i o", o=D)
        full = INTER // 128
        w(dn[:, 0:full, :], a["downT"][0:full * 128, :].rearrange("(i p) o -> p i o", p=128))
        w(dn[0:INTER - full * 128, full, :], a["downT"][full * 128:INTER, :])
        assert n[0] == N_DMA

        def load_ctx(l, b):
            pl, v = count_before(l, b, 6, 5)
            hold(c_lo[pl], v)
            src = a["ctxT"][b].rearrange("(k p) t -> p k t", p=128)
            sp.dma_start(ctx_t[:, :, 0:T], src).then_inc(ctx_ready[l], 16)
            sp.dma_start(ctx_t[:, :, T:TP], src[:, :, 0:TP - T]).then_inc(ctx_ready[l], 16)

        def load_qhat(l, b):
            hold(dv["q0lo" if l == 0 else "q1lo"], b + 1)
            hold(sc_done[l], b * G)
            if isinstance(b, int) and b == 0:
                sp.wait_ge(const_ready, N_CONST)
            for s in range(2):
                for r, part in enumerate((0, 0, 1)):
                    p = 64 * s + HD * r
                    sp.dma_start(qhat[l][p:p + HD, :, s, :], q_parts[l][:, s, part, :]).then_inc(qhat_ready[l], 16)
                p = 64 * s + 3 * HD
                sp.dma_start(qhat[l][p:p + 3, :, s, :], zeros3[:, :, :]).then_inc(qhat_ready[l], 16)

        def load_khat(l, b):
            for i in range(6):
                s, c = i // 3, i % 3
                hold(kv_lo[l], b * 12 + i + 1)
                if i == 0:
                    hold(sc_done[l], b * G)
                    if isinstance(b, int) and b == 0:
                        sp.wait_ge(const_ready, N_CONST)
                        if l == 1:
                            sp.wait_ge(lut_done, 1)
                for r, part in enumerate((0, 1, 0)):
                    p = 64 * s + HD * r
                    sp.dma_start(khat[l][p:p + HD, :, c * 512:c * 512 + 512],
                                 k_parts[:, s, part, c * 512:c * 512 + 512]).then_inc(khat_ready[l], 16)

        def load_max(l, b, h):
            hold(m_split[h][l], b + 1)
            hold(m_mm[l], b * 48 + 24 * (h + 1))
            for s in range(2):
                p = 64 * s + 3 * HD
                sp.dma_start(qhat[l][p:p + 3, 4 * h:4 * h + 4, s, :],
                             m_parts[h][12 * s:12 * s + 12, :]).then_inc(m_rows[h][l], 16)

        def slot_a(b):
            side, post, prep = b - 1, b - 2, b + 1
            if exists(side):
                load_qhat(1, side)
            if exists(prep):
                load_ctx(0, prep)
            if exists(side):
                hold(flag_ready, side + 1)
                flag = sp.value_load(mask_flag[0:1, 0:1], min_val=0, max_val=1)
                hold(sc_done[1], side * G)
                with sp.If(flag > 0):
                    sp.dma_start(mask_sb[:, 0:T], a["mask"][side]).then_inc(mask_ready, 16)
                with sp.Else():
                    sp.sem_inc(mask_ready, 16)
                load_khat(1, side)
            if exists(b):
                hold(dv["x1"], b)
                sp.dma_start(x_res[:, :], a["x"][b]).then_inc(x_res_in, 16)
            if exists(post):
                hold(dv["x3"], post + 1)
                sp.dma_start(x3_dram[post], x3[:, :]).then_inc(x3_out, 16)
            if exists(b):
                load_max(0, b, 1)
            if exists(side):
                load_max(1, side, 0)

        def slot_b(b):
            main, side = b - 1, b + 1
            if exists(side):
                load_qhat(0, side)
            if exists(b + 2):
                hold(dv["y0"], b + 2)
                sp.dma_start(x_q[:, :], a["x"][b + 2]).then_inc(x_q_in, 16)
            if exists(b):
                hold(chk_abs, 3 * b)
                sp.dma_start(mask_chk[:, :], a["mask"][b]).then_inc(chk_in, 16)
                load_ctx(1, b)
            if exists(b - 1):
                hold(dv["x3"], b - 1)
                hold(x2_out, 16 * b)
                sp.dma_start(x2_in[:, :], x2_dram[b - 1]).then_inc(x2_in_s, 16)
            if exists(side):
                load_khat(0, side)
            if exists(main):
                load_max(1, main, 1)
            if exists(b):
                hold(dv["x2"], b + 1)
                sp.dma_start(x2_dram[b], x2[:, :]).then_inc(x2_out, 16)
            if exists(side):
                load_max(0, side, 0)

        sp.dma_start(x_q[:, :], a["x"][0]).then_inc(x_q_in, 16)
        load_ctx(0, 0)
        slot_b(-1)
        for b in range(FIRST):
            slot_a(b)
            slot_b(b)
        with sp.Fori(FIRST, LAST_IT) as b:
            slot_a(b)
            slot_b(b)
        for b in range(LAST_IT, B + 1):
            slot_a(b)
            slot_b(b)
        slot_a(B + 1)

        sp.wait_ge(x3_out, 16 * B)
        sp.dma_start(X[:, :, :], x3_dram.rearrange("b q d -> q b d")).then_inc(x_in, 16)
        for dst, src in ((wr[:, :, :], a["Wr"].rearrange("(k p) e -> p k e", p=128)),
                         (br_r[:, :], rows(a["br"], S)), (b2_s[:, :], a["b2"]),
                         (wp1[:, :, :], a["Wp1"].rearrange("(k p) o -> p k o", p=128)),
                         (bp1[:, :], a["bp1"]), (wp2[:, :], a["Wp2"]), (bp2_r[:, :], rows(a["bp2"], S))):
            sp.dma_start(dst, src).then_inc(e_in, 16)

        def expert(n, p):
            hold(w_lo, 2 * n)
            if not isinstance(n, int):
                hold(h_done, (n - 1) * HT * 8)
            sp.dma_start(w_stage2[0][:, :].rearrange("p (k h) -> p k h", k=2),
                         a["w1"][n].rearrange("(k p) o -> p k o", p=128)).then_inc(w_in, 16)
            sp.dma_start(w_stage2[1][:, :].rearrange("p (k o) -> p k o", k=HT),
                         a["w2"][n].rearrange("(k p) o -> p k o", p=128)).then_inc(w_in, 16)
            sp.dma_start(b1[p][:, :], a["b1"][n]).then_inc(w_in, 16)

        for p in range(2):
            expert(p, p)
        with sp.Fori(1, E // 2) as i:
            for p in range(2):
                expert(2 * i + p, p)
        for c in range(4):
            sp.wait_ge(e["final"], c + 1)
            sp.dma_start(out[8 * c:8 * c + 8].rearrange("b q d -> q b d"), acc[:, 8 * c:8 * c + 8, :]).then_inc(out_sem, 16)
        sp.wait_ge(out_sem, 64)

    @block.tensor
    def _(te):
        te.wait_ge(const_ready, N_CONST)
        te.wait_ge(attn_weights, 16 * N_DMA)
        te.wait_ge(wq_int, 1)
        for m in range(2):
            for c in range(2):
                for k in range(2):
                    te.transpose(chb[:, (m * 2 + c) * D + k * 128:(m * 2 + c) * D + k * 128 + 128],
                                 w_int[:, m, k, c * 128:c * 128 + 128], identb[:, :])
        for m in range(2):
            for k in range(2):
                last = te.matmul(kv_bank[0:S, m * D + k * 128:m * D + k * 128 + 128],
                                 w_sb[:, 2 * m + k, :], ident[:, :], start=True, stop=True)
        last.then_inc(wq_tr, 1)
        te.wait_ge(wq_ready, 2)

        def scores(l, b, g, masked):
            j, t = group(g)
            if g >= 2:
                te.wait_ge(exp_done[l], b * G + g - 1)
            else:
                pl, v = count_before(l, b, G, G - 2 + g)
                wait(te, exp_done[pl], v)
            if g == 0:
                te.wait_ge(qhat_ready[l], 16 * 8 * (b + 1))
                te.wait_ge(khat_ready[l], 16 * 18 * (b + 1))
            if g % (G // 2) == 0:
                te.wait_ge(m_rows[g // (G // 2)][l], 16 * 2 * (b + 1))
            for n in range(2):
                o = sc_bank[g % 2][:, n * 2 * S:(n + 1) * 2 * S]
                if masked:
                    te.matmul(o, mask_sb[:, (t + n) * 128:(t + n + 1) * 128], ident2[:, :], start=True, stop=False)
                last = te.matmul(o, khat[l][:, j, (t + n) * 128:(t + n + 1) * 128],
                                 qhat[l][:, j, :, :].rearrange("p s q -> p (s q)"), start=not masked, stop=True)
            last.then_inc(sc_done[l], 1)

        def values(l, b, g):
            j, t = group(g)
            te.wait_ge(res_done[l], b * G + g + 1)
            if g % (KT // 2) == 0:
                if j >= 2:
                    te.wait_ge(o_evac[l], b * NP + j - 1)
                else:
                    pl, v = count_before(l, b, NP, NP - 2 + j)
                    wait(te, o_evac[pl], v)
            pb = probs[:, g % 4, :].bitcast(BF16)
            for s in range(2):
                o = o_bank[j % 2][:, s * VW:(s + 1) * VW]
                for n in range(2):
                    r = LAST if t + n == KT - 1 else 128
                    c = (2 * n + s) * S
                    v = vhat[l][0:r, t + n, s * NP + j, :]
                    te.matmul(o, pb[0:r, 2 * c + 1:2 * c + 256:2], v, start=(t + n == 0 and s == 0),
                              stop=False, skip_group_check=True)
                    last = te.matmul(o, rest[0:r, g % 4, c:c + 128], v, start=False,
                                     stop=(t + n == KT - 1), skip_group_check=True)
            last.then_inc(pv_done[l], 1)

        def chunk(l, b, i, half):
            if half == 0 and i == 0:
                te.wait_ge(c_lo[l], 6 * (b + 1))
                pl, v = count_before(l, b, 12, 11)
                wait(te, kv_lo[pl], v)
            elif half == 0:
                te.wait_ge(kv_lo[l], b * 12 + i)
            if i < 6:
                s, c = i // 3, i % 3
                for n, (k, pw, pc) in list(enumerate(TERMS))[3 * half:3 * half + 3]:
                    last = te.matmul(kv_bank[:, :], wk[l][:, pw, k, s * 128:s * 128 + 128],
                                     c_parts[:, pc, k, c * 512:c * 512 + 512], start=(n == 0), stop=(n == 5))
            else:
                t = 2 * (i - 6) + half
                for n, (k, pw, pc) in enumerate(TERMS):
                    last = te.matmul(kv_bank[:, half * D:(half + 1) * D], c_parts[:, pc, k, t * 128:t * 128 + 128],
                                     wv[l][:, pw, k, :], start=(n == 0), stop=(n == 5))
            if half:
                last.then_inc(kv_mm[l], 1)

        def maxima(l, b, u, masked):
            hu, c = u // 3, u % 3
            j, s = hu // 2, hu % 2
            n = min(MC, T - c * MC)
            if u == 0:
                te.wait_ge(qhat_ready[l], 16 * 8 * (b + 1))
                te.wait_ge(khat_ready[l], 16 * 18 * (b + 1))
                if masked:
                    te.wait_ge(mask_ready, 16 * (b + 1))
            if u >= 2:
                te.wait_ge(m_red[l], b * 48 + u - 1)
            else:
                pl, v = count_before(l, b, 48, 46 + u)
                wait(te, m_red[pl], v)
            o = mx_bank[u % 2][0:S, 0:n]
            if masked:
                te.matmul(o, ident[0:S, 0:S], mask_sb[:, c * MC:c * MC + n], start=True, stop=False)
            te.matmul(o, qhat[l][:, j, s, :], khat[l][:, j, c * MC:c * MC + n],
                      start=not masked, stop=True).then_inc(m_mm[l], 1)

        def max_turn(l, b, h):
            te.wait_ge(m_fold[h][l], b + 1)
            te.transpose(chb[0:24, 0:S], m_nat[h][:, :, :, :].rearrange("q s k j -> q (s k j)"),
                         identb[0:S, 0:S]).then_inc(m_tr[h][l], 1)

        def turn(src, key, to=None, idn=None):
            for k in range(2):
                last = te.transpose((to or ch)[:, k * S:(k + 1) * S], src[:, k * 128:k * 128 + 128],
                                    (idn or ident)[0:S, 0:S])
            last.then_inc(pe[key], 1)

        def product(xT, wt, key, n=2):
            for k in range(n):
                last = te.matmul(ch[0:S, 0:D], xT[:, k, :], wt[:, k, :], start=(k == 0), stop=(k == n - 1))
            last.then_inc(pe[key], 1)

        def chain_a(b, g):
            post, prep = b - 2, b + 1
            if exists(post):
                if g == 12:
                    te.wait_ge(dv["o1i"], post + 1)
                    if exists(prep):
                        te.wait_ge(dv["q0lo"], prep + 1)
                    turn(q_int, "o1T", chb, identb)
                if g == 14:
                    te.wait_ge(cp["o1T"], post + 1)
                    product(qT, wo1, "wo1")
            if exists(prep):
                if g == 5:
                    te.wait_ge(dv["y0"], prep + 1)
                    turn(y, "q0T")
                if g == 7:
                    te.wait_ge(cp["q0T"], prep + 1)
                    product(yT, wq0, "q0")
                if g == 9:
                    te.wait_ge(dv["q0n"], prep + 1)
                    turn(q_nat, "q0N")

        def chain_b(b, g):
            if not exists(b):
                return
            if g == 7:
                te.wait_ge(o_norm[0], b + 1)
                turn(o_n, "oT")
            if g == 9:
                te.wait_ge(cp["oT"], b + 1)
                product(yT, wo0, "wo")
            if g == 15:
                te.wait_ge(dv["y1"], b + 1)
                turn(y, "y1T")
            if g in FFN_AT:
                f = FFN_AT.index(g)
                if f == 0:
                    te.wait_ge(cp["y1T"], b + 1)
                    if isinstance(b, int) and b == 0:
                        te.wait_ge(lut_done, 1)
                else:
                    te.wait_ge(cp[f"ffn{f - 1}"], b + 1)
                if f == 0 and exists(b - 1):
                    te.wait_ge(m_split[1][1], b)
                for n in range(2):
                    for m, wt in enumerate((gate_w, up_w)):
                        for k in range(2):
                            last = te.matmul(ch[:, (2 * n + m) * S:(2 * n + m + 1) * S],
                                             wt[:, k, (2 * f + n) * 128:(2 * f + n + 1) * 128], yT[:, k, :],
                                             start=(k == 0), stop=(k == 1))
                last.then_inc(pe[f"ffn{f}"], 1)
            if g == 28:
                te.wait_ge(dv["h2"], b + 1)
                product(hbuf, down_w, "down", IT)
            if g == 36:
                te.wait_ge(dv["q1i"], b + 1)
                turn(q_int, "q1T", chb, identb)
            if g == 37:
                te.wait_ge(cp["q1T"], b + 1)
                product(qT, wq1, "q1")
            if g == 43:
                te.wait_ge(dv["q1n"], b + 1)
                if exists(b + 1):
                    te.wait_ge(m_split[0][0], b + 2)
                turn(q_nat, "q1N")
            if g == 40:
                te.wait_ge(chk_abs, 3 * b + 3)
                if exists(b + 1):
                    te.wait_ge(kv_lo[0], 12 * (b + 2))
                te.matmul(kv_bank[0:1, 0:3], ones_col[0:S, :], mask_abs[:, :], start=True, stop=True).then_inc(flag_mm, 1)

        def slot(prev, main, side, chain, b, masked):
            (pl, pb), (ml, mb), (sl, sb_) = prev, main, side
            b_chain = chain is chain_b
            for g in range(G):
                if exists(mb):
                    scores(ml, mb, g, masked and ml == 1)
                if exists(sb_) and g - 1 in CHUNK:
                    chunk(sl, sb_, CHUNK[g - 1], 1)
                if exists(pb) and g < LAG:
                    values(pl, pb, G - LAG + g)
                if exists(mb) and g >= LAG:
                    values(ml, mb, g - LAG)
                for job, units in ((main, UNITS[ml][0]), (side, UNITS[sl][1])):
                    if exists(job[1]):
                        for u in units[g]:
                            maxima(*job, u, masked and job[0] == 1)
                if exists(mb) and g == TURN_1:
                    if b_chain and exists(b):
                        te.wait_ge(cp["y1T"], b + 1)
                    max_turn(ml, mb, 1)
                if exists(sb_):
                    if g in CHUNK:
                        chunk(sl, sb_, CHUNK[g], 0)
                    if g == TURN_0:
                        if b_chain and exists(b):
                            te.wait_ge(dv["q1n"], b + 1)
                        max_turn(sl, sb_, 0)
                chain(b, g)

        def slots(b, masked):
            slot((1, b - 2), (0, b), (1, b - 1), chain_a, b, masked)
            slot((0, b), (1, b - 1), (0, b + 1), chain_b, b, masked)

        def iteration(b):
            if not exists(b - 1):
                slots(b, False)
                return
            te.wait_ge(flag_ready, b)
            te.sem_inc(tick, 1)
            flag = te.value_load(mask_flag[0:1, 0:1], min_val=0, max_val=1)
            with te.If(flag > 0):
                slots(b, True)
            with te.Else():
                slots(b, False)

        for b in range(-1, FIRST):
            iteration(b)
        with te.Fori(FIRST, LAST_IT) as b:
            iteration(b)
        for b in range(LAST_IT, B + 2):
            iteration(b)

        te.wait_ge(e["y"], 1)
        for b in range(B):
            wait(te, e["yT"], b - 3)
            for k in range(2):
                last = te.transpose(bank[b % 4][:, k * S:(k + 1) * S], Y[:, b, k * 128:k * 128 + 128], ident[0:S, 0:S])
            last.then_inc(e["yT_mm"], 1)
        te.wait_ge(e_in, 16 * N_SMALL)
        te.wait_ge(e["yT"], B)
        for b in range(B):
            for k in range(2):
                last = te.matmul(bank[4][0:S, b * E:(b + 1) * E], YT[:, k, b * S:(b + 1) * S], wr[:, k, :],
                                 start=(k == 0), stop=(k == 1))
        last.then_inc(e["logits"], 1)
        te.wait_ge(e["sums_in"], 1)
        te.matmul(bank[5][0:S, 0:2 * E], onesS[:, :], cms[:, :, :].rearrange("p a e -> p (a e)"),
                  start=True, stop=True).then_inc(e["sums"], 1)
        te.wait_ge(e["gates"], 1)
        for b in range(B):
            if b % 4 == 0:
                wait(te, e["gT"], b // 4 - 1)
            last = te.transpose(bank[b // 4 % 2][0:E, (b % 4) * S:(b % 4 + 1) * S], gt[:, :, b], ident[0:S, 0:S])
            if b % 4 == 3:
                last.then_inc(e["gT_mm"], 1)
        for b in range(B):
            if b % 4 == 0:
                te.wait_ge(e["gT"], b // 4 + 1)
            if b % 2 == 0:
                wait(te, e["init"], b // 2 - 1)
            last = te.matmul(bank[6 + b // 2 % 2][0:S, (b % 2) * D:(b % 2 + 1) * D], gT[:, b, :], b2_s[:, :],
                             start=True, stop=True)
            if b % 2 == 1:
                last.then_inc(e["init_mm"], 1)
        te.wait_ge(e["init"], B // 2)

        def hidden(n, p, tb):
            for i in range(HT):
                m = tb * HT + i
                wait(te, h_done, n * 40 + m - 3)
                for j, (k, pw, py) in enumerate(TERMS):
                    last = te.matmul(bank[m % 4][:, 0:4 * S], w1p[p][:, pw, k, i * 128:i * 128 + 128],
                                     y_parts[:, py, k, tb * 4 * S:(tb + 1) * 4 * S], start=(j == 0), stop=(j == 5))
                last.then_inc(h_mm, 1)

        def back(n, p, tb):
            te.wait_ge(r_done, n * 40 + tb * HT + HT)
            hi = hid[tb % 2][:, :, :].bitcast(BF16)[:, :, 1:8 * S:2]
            for q in range(4):
                b = tb * 4 + q
                wait(te, y_acc, n * B + b - 3)
                for i in range(HT):
                    for j, (h, pw) in enumerate(((hi, 0), (hi, 1), (hid_lo[tb % 2], 0))):
                        last = te.matmul(bank[4 + q][0:S, 0:D], h[:, i, q * S:(q + 1) * S], w2p[p][:, pw, i, :],
                                         start=(i == 0 and j == 0), stop=(i == HT - 1 and j == 2))
                last.then_inc(y_mm, 1)

        def experts(i):
            for p in range(2):
                n = 2 * i + p
                te.wait_ge(w_lo, 2 * n + 2)
                for tb in range(8):
                    if isinstance(n, int) and n == 0:
                        te.wait_ge(y_lo, tb + 1)
                    hidden(n, p, tb)
                    if tb:
                        back(n, p, tb - 1)
                back(n, p, 7)

        experts(0)
        with te.Fori(1, E // 2) as i:
            experts(i)
        te.wait_ge(y_acc, E * B)
        for k in range(2):
            for b in range(B):
                last = te.matmul(bank[0][:, k * B + b:k * B + b + 1], acc[:, b, k * 128:k * 128 + 128],
                                 onesS[:, 0:1], start=True, stop=True)
        last.then_inc(e["phi_mm"], 1)
        te.wait_ge(e["phi"], 1)
        for k in range(2):
            last = te.matmul(bank[1][:, 0:B], wp1[:, k, :], pooled[:, k, :], start=(k == 0), stop=(k == 1))
        last.then_inc(e["phi_mm"], 1)
        te.wait_ge(e["phi"], 2)
        te.wait_ge(e["small"], 1)
        te.matmul(bank[2][0:S, 0:B], wp2b[:, :], hp[:, :], start=True, stop=True).then_inc(e["phi_mm"], 1)

    @block.scalar
    def _(ac):
        ac.wait_ge(wq_tr, 1)
        for m, dst in ((0, wq1), (1, wo1)):
            last = nc.scalar.activation(dst[:, :, :].rearrange("p c o -> p (c o)"), chb[:, m * 2 * D:(m + 1) * 2 * D], ACT.Copy)
        last.then_inc(wq_ready, 1)

        def exps(l, b, g):
            ac.wait_ge(sc_done[l], b * G + g + 1)
            if g >= 4:
                ac.wait_ge(pv_done[l], b * G + g - 3)
            else:
                pl, v = count_before(l, b, G, G - 4 + g)
                wait(ac, pv_done[pl], v)
            nc.scalar.activation(probs[:, g % 4, 0:4 * S], sc_bank[g % 2][:, 0:4 * S], ACT.Exp).then_inc(exp_done[l], 1)

        def evac(l, b, j):
            if j == 0:
                wait(ac, o_norm[l], b)
            ac.wait_ge(pv_done[l], b * G + (KT // 2) * (j + 1))
            nc.scalar.activation(o_raw[l][:, j, :, :].rearrange("p s c -> p (s c)"),
                                 o_bank[j % 2][0:S, 0:2 * VW], ACT.Copy).then_inc(o_evac[l], 1)

        def high(l, b, i):
            ac.wait_ge(kv_mm[l], b * 12 + i + 1)
            if i < 6:
                s, c = i // 3, i % 3
                if c == 0:
                    pl, v = count_before(l, b, 16 * 18, 16 * 18 - 1)
                    wait(ac, khat_ready[pl], v)
                nc.scalar.activation(k_parts[:, s, 0, c * 512:c * 512 + 512], kv_bank[:, :], ACT.Identity,
                                     bias=bk[l][:, s:s + 1]).then_inc(kv_hi[l], 1)
            else:
                t = 2 * (i - 6)
                wait(ac, pv_done[l], b * G)
                nc.scalar.activation(vhat[l][:, t:t + 2, :, 0:HD],
                                     kv_bank[:, :].rearrange("p (n h d) -> p n h d", n=2, h=H),
                                     ACT.Copy).then_inc(kv_hi[l], 1)

        def c_high(l, b, i):
            c, k = i // 2, i % 2
            if i == 0:
                ac.wait_ge(ctx_ready[l], 32 * (b + 1))
            if k == 0:
                pl, v = count_before(l, b, 12, 7 + 2 * c)
                wait(ac, kv_mm[pl], v)
            nc.scalar.activation(c_parts[:, 0, k, c * 512:c * 512 + 512], ctx_t[:, k, c * 512:c * 512 + 512],
                                 ACT.Copy).then_inc(c_hi[l], 1)

        def copy_T(key, b, dst, src=None):
            ac.wait_ge(pe[key], b + 1)
            nc.scalar.activation(dst[:, :, :].rearrange("p k q -> p (k q)"), (ch if src is None else src)[:, 0:2 * S],
                                 ACT.Copy).then_inc(cp[key], 1)

        def q_high(l, key, b):
            ac.wait_ge(pe[key], b + 1)
            wait(ac, qhat_ready[l], 16 * 8 * b)
            nc.scalar.activation(q_parts[l][:, :, 0, :], ch[:, 0:2 * S].rearrange("p (s q) -> p s q", s=2),
                                 ACT.Copy, scale=1.0 / HD ** 0.5).then_inc(cp[key], 1)

        def chain_a(b, g):
            post, prep = b - 2, b + 1
            if exists(post) and g == 13:
                copy_T("o1T", post, qT, chb)
            if exists(prep):
                if g == 6:
                    copy_T("q0T", prep, yT)
                if g == 10:
                    q_high(0, "q0N", prep)

        def chain_b(b, g):
            if not exists(b):
                return
            if g == 8:
                copy_T("oT", b, yT)
            if g == 16:
                copy_T("y1T", b, yT)
            if g - 1 in FFN_AT:
                f = FFN_AT.index(g - 1)
                ac.wait_ge(pe[f"ffn{f}"], b + 1)
                if f == 2:
                    ac.wait_ge(dv["h0"], b + 1)
                else:
                    wait(ac, dv["h2" if f == 0 else "h1"], b)
                nc.scalar.activation(ex[f % 2][:, :, :], ch[:, 0:4 * S].rearrange("p (n m q) -> p n m q", n=2, m=2)[:, :, 0, :],
                                     ACT.Exp, scale=-1.0)
                nc.scalar.activation(gu[f % 2][:, :, :, :].rearrange("p n m q -> p (n m q)"), ch[:, 0:4 * S],
                                     ACT.Copy).then_inc(cp[f"ffn{f}"], 1)
            if g == 37:
                copy_T("q1T", b, qT, chb)
            if g == 44:
                q_high(1, "q1N", b)

        def slot(prev, main, side, chain, b):
            (pl, pb), (ml, mb), (sl, sb_) = prev, main, side
            for g in range(G):
                if exists(mb):
                    exps(ml, mb, g)
                if exists(sb_) and g - 1 in CHUNK:
                    high(sl, sb_, CHUNK[g - 1])
                if exists(pb) and g == LAG:
                    evac(pl, pb, NP - 1)
                if exists(mb) and g >= 9 and (g - 9) % 6 == 0:
                    evac(ml, mb, (g - 9) // 6)
                chain(b, g)
                if exists(mb + 1) and g in SPLITS:
                    c_high(ml, mb + 1, SPLITS[g])

        def slot_a(b):
            slot((1, b - 2), (0, b), (1, b - 1), chain_a, b)

        def slot_b(b):
            slot((0, b), (1, b - 1), (0, b + 1), chain_b, b)

        slot_a(-1)
        slot_b(-1)
        for b in range(FIRST):
            slot_a(b)
            slot_b(b)
        with ac.Fori(FIRST, LAST_IT) as b:
            slot_a(b)
            slot_b(b)
        for b in range(LAST_IT, B + 1):
            slot_a(b)
            slot_b(b)
        slot_a(B + 1)

        for b in range(B):
            ac.wait_ge(e["yT_mm"], b + 1)
            nc.scalar.activation(YT[:, :, b * S:(b + 1) * S], bank[b % 4][:, 0:2 * S].rearrange("p (k q) -> p k q", k=2),
                                 ACT.Copy).then_inc(e["yT"], 1)
        for tb in range(8):
            if tb == 0:
                ac.wait_ge(e["yT"], B)
            t = slice(tb * 4 * S, (tb + 1) * 4 * S)
            nc.scalar.activation(y_parts[:, 0, :, t], YT[:, :, t], ACT.Copy).then_inc(y_hi, 1)

        def w_high(n, p, m):
            ac.wait_ge(w_in, 48 * (n + 1))
            wait(ac, y_mm, (n - 1) * B)
            nc.scalar.activation(w_parts[p][m][:, 0, :], w_stage2[m][:, :], ACT.Copy).then_inc(w_hi, 1)

        for m in range(2):
            w_high(0, 0, m)
        ac.wait_ge(e["exp_in"], 1)
        nc.scalar.activation(pr[:, :, :], lg[:, :, :], ACT.Exp).then_inc(e["exp"], 1)
        ac.wait_ge(e["exp_in"], 2)
        nc.scalar.activation(ex3[:, :, :], ew[:, :, :], ACT.Exp).then_inc(e["exp"], 1)
        for c in range(B // 4):
            ac.wait_ge(e["gT_mm"], c + 1)
            nc.scalar.activation(gT[:, 4 * c:4 * c + 4, :].rearrange("e b q -> e (b q)"), bank[c % 2][0:E, 0:4 * S],
                                 ACT.Copy).then_inc(e["gT"], 1)
        for c in range(B // 2):
            ac.wait_ge(e["init_mm"], c + 1)
            nc.scalar.activation(acc[:, 2 * c:2 * c + 2, :].rearrange("q b d -> q (b d)"), bank[6 + c % 2][0:S, :],
                                 ACT.Copy).then_inc(e["init"], 1)

        def experts(i, last=False):
            for p in range(2):
                n = 2 * i + p
                for tb in range(8):
                    if tb in W_AT and not (last and p == 1):
                        w_high(n + 1, 1 - p, W_AT.index(tb))
                    wait(ac, y_mm, n * B + (tb - 1) * 4)
                    for k in range(HT):
                        m = tb * HT + k
                        ac.wait_ge(h_mm, n * 40 + m + 1)
                        nc.scalar.activation(hid[tb % 2][:, k, :], bank[m % 4][:, 0:4 * S], ACT.Relu,
                                             bias=b1[p][:, k:k + 1]).then_inc(h_done, 1)

        experts(0)
        with ac.Fori(1, E // 2 - 1) as i:
            experts(i)
        experts(E // 2 - 1, True)
        ac.wait_ge(e["phi_mm"], 1)
        nc.scalar.activation(pooled[:, :, :].rearrange("p k b -> p (k b)"), bank[0][:, 0:2 * B], ACT.Copy,
                             scale=1.0 / S).then_inc(e["phi"], 1)
        ac.wait_ge(e["phi_mm"], 2)
        nc.scalar.activation(hp[:, :], bank[1][:, 0:B], ACT.Relu, bias=bp1[:, 0:1]).then_inc(e["phi"], 1)
        ac.wait_ge(e["phi_mm"], 3)
        nc.scalar.activation(fac[:, :], bank[2][0:S, 0:B], ACT.Exp, scale=-1.0, bias=nbp2[:, 0:1]).then_inc(e["phi"], 1)

    @block.gpsimd
    def _(po):
        po.memset(ident[:, :], 0.0).then_inc(pool_pro, 1)
        po.memset(identb[:, :], 0.0).then_inc(pool_pro, 1)
        po.wait_ge(pool_pro, 2)
        for m in (ident, identb):
            po.affine_select(out=m[:, :], in_=m[:, :], compare_op=ALU.not_equal, fill=1.0, base=0,
                             pattern=[[-1, 128]], channel_multiplier=1).then_inc(pool_pro, 1)
        po.wait_ge(pool_pro, 4)
        for l in range(2):
            po.memset(vhat[l][:, :, :, VW - 1:VW], 1.0).then_inc(const_ready, 1)
            po.memset(qhat[l][:, :, :, :], 0.0).then_inc(const_ready, 1)
        po.memset(probs[:, :, 4 * S:432], 0.0).then_inc(const_ready, 1)
        po.memset(rest[:, :, 4 * S:432], 0.0).then_inc(const_ready, 1)
        po.memset(mask_sb[:, T:TP], 0.0).then_inc(const_ready, 1)
        po.memset(zeros3[:, :, :], 0.0).then_inc(const_ready, 1)
        po.memset(half_neg[:, :], -0.5).then_inc(const_ready, 1)
        po.wait_ge(w_split, 1)
        po.memset(khat[0][:, :, :], 1.0).then_inc(const_ready, 1)

        def residual(l, b, g):
            po.wait_ge(exp_done[l], b * G + g + 1)
            hi = probs[:, g % 4, :].bitcast(BF16)[:, 1:2 * 4 * S:2]
            po.tensor_tensor(rest[:, g % 4, 0:4 * S], probs[:, g % 4, 0:4 * S], hi, ALU.subtract).then_inc(res_done[l], 1)

        def power(key, b):
            po.wait_ge(ln_var[key], b + 1)
            po.tensor_tensor(rstd[:, :], veps[:, :], half_neg[0:S, 0:1], ALU.pow).then_inc(ln_rstd[key], 1)

        def chain_a(b, g):
            if exists(b + 1) and g == 3:
                power("q0", b + 1)

        def chain_b(b, g):
            if exists(b):
                if g == 13:
                    power("ffn", b)
                if g == 31:
                    power("q1", b)

        def slot(main, chain, b):
            for g in range(G):
                if exists(main[1]):
                    residual(main[0], main[1], g)
                chain(b, g)

        for g in range(G):
            chain_a(-1, g)
        slot((1, -2), chain_b, -1)
        for b in range(FIRST):
            slot((0, b), chain_a, b)
            slot((1, b - 1), chain_b, b)
        with po.Fori(FIRST, LAST_IT) as b:
            slot((0, b), chain_a, b)
            slot((1, b - 1), chain_b, b)
        for b in range(LAST_IT, B + 1):
            slot((0, b), chain_a, b)
            slot((1, b - 1), chain_b, b)
        slot((0, B + 1), chain_a, B + 1)
        po.wait_ge(e["var"], 1)
        po.tensor_tensor(rst[:, :], var[:, :], half_neg[0:S, 0:B], ALU.pow).then_inc(e["rstd"], 1)

        def w_low(n, p, m):
            wait(po, w_hi, 2 * n + m + 1)
            po.tensor_tensor(w_parts[p][m][:, 1, :], w_stage2[m][:, :], w_parts[p][m][:, 0, :], ALU.subtract).then_inc(w_lo, 1)

        for tb in range(8):
            t = slice(tb * 4 * S, (tb + 1) * 4 * S)
            po.wait_ge(y_hi, tb + 1)
            po.tensor_tensor(y_parts[:, 1, :, t], YT[:, :, t], y_parts[:, 0, :, t], ALU.subtract).then_inc(y_lo, 1)
        for m in range(2):
            w_low(0, 0, m)

        def experts(i, last=False):
            for p in range(2):
                n = 2 * i + p
                for tb in range(8):
                    if tb in W_AT and not (last and p == 1):
                        w_low(n + 1, 1 - p, W_AT.index(tb))
                    for k in range(HT):
                        po.wait_ge(h_done, n * 40 + tb * HT + k + 1)
                        hi = hid[tb % 2][:, k, :].bitcast(BF16)[:, 1:8 * S:2]
                        po.tensor_tensor(hid_lo[tb % 2][:, k, :], hid[tb % 2][:, k, :], hi, ALU.subtract).then_inc(r_done, 1)

        experts(0)
        with po.Fori(1, E // 2 - 1) as i:
            experts(i)
        experts(E // 2 - 1, True)

    @block.vector
    def _(ve):
        k = [0]

        def link(ins):
            k[0] += 1
            ins.then_inc(dve_link, 1)
            ve.wait_ge(dve_link, k[0])

        ve.wait_ge(pool_pro, 4)
        for i in range(2):
            ve.tensor_copy(ident2[:, i * S:(i + 1) * S], ident[0:S, 0:S]).then_inc(const_ready, 1)
        ve.memset(ones_col[:, :], 1.0).then_inc(const_ready, 1)
        ve.wait_ge(attn_weights, 16 * N_DMA)
        for l in range(2):
            for m, dst in enumerate((wk[l], wv[l])):
                link(ve.tensor_copy(dst[:, 0, :, :], w_stage[2 * l + m]))
                last = ve.tensor_tensor(dst[:, 1, :, :], w_stage[2 * l + m], dst[:, 0, :, :], ALU.subtract)
        last.then_inc(w_split, 1)
        link(ve.tensor_reduce(w_amax[:, :].rearrange("p (m k) -> p m k", m=2), w_nat[:, :, :, :], AX.X, ALU.max,
                              apply_absolute_value=True))
        link(ve.tensor_scalar(w_s[:, :], w_amax[:, :], 1.0 / 127.0, EPS_Q, ALU.mult, ALU.max))
        link(ve.reciprocal(w_rs[:, :], w_s[:, :]))
        for r in range(4):
            m, c = r // 2, r % 2
            link(ve.tensor_scalar(w_t[:, m, c, :], w_nat[:, m, c, :], w_rs[:, r:r + 1], MAGIC, ALU.mult, ALU.add))
        wt = w_t.rearrange("p m k c -> p m (k c)")
        link(ve.tensor_scalar(wt, wt, -MAGIC, 127.0, ALU.add, ALU.min))
        link(ve.tensor_scalar(w_int.rearrange("p m k c -> p m (k c)"), wt, -127.0, None, ALU.max))
        ve.tensor_copy(w_sb[:, :, :], w_s[:, :].rearrange("p (r u) -> p r u", u=1).to_broadcast([128, 4, S])).then_inc(wq_int, 1)
        ve.wait_ge(wq_tr, 1)
        for m in range(2):
            last = ve.tensor_copy(sw_r[m][:, :], kv_bank[0:S, m * D:(m + 1) * D])
        last.then_inc(wq_ready, 1)
        for w in (gate_w, up_w, down_w):
            link(ve.memset(w[:, :, :], 0.0))
        dn = idx_d.rearrange("p j c -> p (j c)").rearrange("p (i o) -> p i o", o=D)
        tm = term.rearrange("p j c -> p (j c)").rearrange("p (i o) -> p i o", o=D)
        full, tail = INTER // 128, INTER % 128
        lookups = ((idx_g[:, :, 0:INTER], term[:, :, 0:INTER], gate_w[:, :, 0:INTER]),
                   (idx_u[:, :, 0:INTER], term[:, :, 0:INTER], up_w[:, :, 0:INTER]),
                   (dn[:, 0:full, :], tm[:, 0:full, :], down_w[:, 0:full, :]),
                   (dn[0:tail, full, :], tm[0:tail, full, :], down_w[0:tail, full, :]))

        def look_up(n):
            (idx, tr, dst), i = lookups[n // LUT], n % LUT
            link(ve.tensor_scalar(tr, idx, float(i), lut_b[0:idx.shape[0], i:i + 1], ALU.is_equal, ALU.mult))
            link(ve.tensor_tensor(dst, dst, tr, ALU.add))
            if n == LOOKUPS - 1:
                ve.memset(khat[1][:, :, :], 1.0).then_inc(lut_done, 1)

        def reduce_unit(l, b, u):
            hu, c = u // 3, u % 3
            j, s = hu // 2, hu % 2
            h, jj = j // 4, j % 4
            ve.wait_ge(m_mm[l], b * 48 + u + 1)
            ve.tensor_reduce(mx3[:, h, s * 4 + jj, c:c + 1], mx_bank[u % 2][0:S, 0:min(MC, T - c * MC)],
                             AX.X, ALU.max).then_inc(m_red[l], 1)

        def fold(l, b, h):
            ln = Link(ve, m_link[l], 10, b, 5 * h)
            ve.wait_ge(m_red[l], b * 48 + 24 * (h + 1))
            part = [m_nat[h][:, :, k, :] for k in range(3)]
            neg, r1 = (t[:, :].rearrange("q (s j) -> q s j", s=2) for t in (m_neg, m_r1))
            ln(lambda: ve.tensor_reduce(mx[:, h, :], mx3[:, h, :, :], AX.X, ALU.max))
            ln(lambda: ve.tensor_scalar(m_neg[:, :], mx[:, h, :], -1.0, None, ALU.mult))
            ln(lambda: ve.tensor_copy(part[0], neg))
            ln(lambda: ve.tensor_tensor(r1, neg, part[0], ALU.subtract))
            ln(lambda: ve.tensor_copy(part[1], r1))
            assert ln.k == 5 * h + 5
            ln.ready()
            ve.tensor_tensor(part[2], r1, part[1], ALU.subtract).then_inc(m_fold[h][l], 1)

        def split(l, b, h):
            ve.wait_ge(m_tr[h][l], b + 1)
            prev = before(l, b)
            if prev is not None:
                wait(ve, m_rows[h][prev[0]], 16 * 2 * (prev[1] + 1))
            ve.tensor_copy(m_parts[h][:, :], chb[0:24, 0:S]).then_inc(m_split[h][l], 1)

        def low(l, b, i):
            ve.wait_ge(kv_hi[l], b * 12 + i + 1)
            if i < 6:
                s, c = i // 3, i % 3
                ve.scalar_tensor_tensor(k_parts[:, s, 1, c * 512:c * 512 + 512], kv_bank[:, :], bk[l][:, s:s + 1],
                                        k_parts[:, s, 0, c * 512:c * 512 + 512], ALU.add, ALU.subtract).then_inc(kv_lo[l], 1)
            else:
                t = 2 * (i - 6)
                ve.tensor_tensor(vhat[l][:, t:t + 2, :, HD:2 * HD], kv_bank[:, :].rearrange("p (n h d) -> p n h d", n=2, h=H),
                                 vhat[l][:, t:t + 2, :, 0:HD], ALU.subtract).then_inc(kv_lo[l], 1)

        def c_low(l, b, i):
            c, k = i // 2, i % 2
            ve.wait_ge(c_hi[l], 6 * b + i + 1)
            ve.tensor_tensor(c_parts[:, 1, k, c * 512:c * 512 + 512], ctx_t[:, k, c * 512:c * 512 + 512],
                             c_parts[:, 0, k, c * 512:c * 512 + 512], ALU.subtract).then_inc(c_lo[l], 1)

        def normalise(ln, l, b, half):
            on = o_n[:, :].rearrange("p (s j d) -> p j s d", s=2, j=NP)
            if half == 0:
                ve.wait_ge(o_evac[l], (b + 1) * NP)
                ln(lambda: ve.reciprocal(rec[:, :, :], o_raw[l][:, :, :, 2 * HD]))
                ln(lambda: ve.tensor_tensor(on, o_raw[l][:, :, :, 0:HD], o_raw[l][:, :, :, HD:2 * HD], ALU.add))
            else:
                ln(lambda: ve.tensor_tensor(on, on, rec[:, :, :].rearrange("p j (s u) -> p j s u", u=1).to_broadcast([S, NP, 2, HD]),
                                            ALU.mult))
                ln.ready()
                ve.tensor_tensor(o_n[:, :], o_n[:, :], bv_r[l][:, :], ALU.add).then_inc(o_norm[l], 1)

        def norm_stats(ln, src):
            ln(lambda: ve.bn_stats(stats[:, :], src[:, :]))

        def norm_var(ln, key):
            ln.ready()
            ve.sem_inc(tick, 1)
            ve.bn_aggr(mv[:, :], stats[:, :]).then_inc(ln.sem, 1)
            ln.k += 1
            ln.ready()
            ve.tensor_scalar(veps[:, :], mv[:, 1:2], EPS_LN, None, ALU.add).then_inc(ln_var[key], 1)

        def norm_apply(src, key, b):
            ve.wait_ge(ln_rstd[key], b + 1)
            return ve.tensor_scalar(y[:, :], src[:, :], mv[:, 0:1], rstd[:, 0:1], ALU.subtract, ALU.mult)

        def quantise(ln, src, done, part):
            if part == 0:
                ln(lambda: ve.tensor_reduce(amax[:, :], src[:, :], AX.X, ALU.max, apply_absolute_value=True))
                ln(lambda: ve.tensor_scalar(s_q[:, :], amax[:, :], 1.0 / 127.0, EPS_Q, ALU.mult, ALU.max))
            elif part == 1:
                ln(lambda: ve.reciprocal(rs_q[:, :], s_q[:, :]))
                ln(lambda: ve.tensor_scalar(t1[:, :], src[:, :], rs_q[:, 0:1], MAGIC, ALU.mult, ALU.add))
            else:
                ln(lambda: ve.tensor_scalar(t1[:, :], t1[:, :], -MAGIC, 127.0, ALU.add, ALU.min))
                ln.ready()
                ve.tensor_scalar(q_int[:, :], t1[:, :], -127.0, None, ALU.max).then_inc(done, 1)

        def q_low(l, key, b, done):
            ve.wait_ge(cp[key], b + 1)
            ve.scalar_tensor_tensor(q_parts[l][:, :, 1, :], ch[:, 0:2 * S].rearrange("p (s q) -> p s q", s=2),
                                    1.0 / HD ** 0.5, q_parts[l][:, :, 0, :], ALU.mult, ALU.subtract).then_inc(done, 1)

        state = {}

        def chain_a(b, g):
            post, prep = b - 2, b + 1
            if exists(prep):
                if g == 1:
                    state["prep"] = Link(ve, lk["qprep0"], 2, prep)
                    ve.wait_ge(x_q_in, 16 * (prep + 1))
                    norm_stats(state["prep"], x_q)
                if g == 2:
                    norm_var(state["prep"], "q0")
                    state["prep"].end()
                if g == 4:
                    norm_apply(x_q, "q0", prep).then_inc(dv["y0"], 1)
                if g == 8:
                    ve.wait_ge(pe["q0"], prep + 1)
                    ve.tensor_tensor(q_nat[:, :], ch[0:S, 0:D], bq_r[0][:, :], ALU.add).then_inc(dv["q0n"], 1)
                if g == 11:
                    q_low(0, "q0N", prep, dv["q0lo"])
            if exists(post):
                if g == 5:
                    state["post"] = Link(ve, lk["post1"], L_POST1, post)
                    normalise(state["post"], 1, post, 0)
                if g == 6:
                    normalise(state["post"], 1, post, 1)
                if g in (7, 9, 10):
                    if g == 7:
                        ve.wait_ge(o_norm[1], post + 1)
                    quantise(state["post"], o_n, dv["o1i"], (7, 9, 10).index(g))
                if g == 15:
                    ve.wait_ge(pe["wo1"], post + 1)
                    state["post"](lambda: ve.scalar_tensor_tensor(t1[:, :], ch[0:S, 0:D], s_q[:, 0:1], sw_r[1][:, :],
                                                                  ALU.mult, ALU.mult))
                    state["post"](lambda: ve.tensor_tensor(t1[:, :], t1[:, :], bo_r[1][:, :], ALU.add))
                if g == 17:
                    state["post"].ready()
                    state["post"].end()
                    ve.wait_ge(x2_in_s, 16 * (post + 1))
                    wait(ve, x3_out, 16 * post)
                    ve.tensor_tensor(x3[:, :], x2_in[:, :], t1[:, :], ALU.add).then_inc(dv["x3"], 1)

        def chain_b(b, g):
            if not exists(b):
                return
            if g == 4:
                state["ln"] = Link(ve, lk["post0"], L_POST0, b)
                normalise(state["ln"], 0, b, 0)
            ln = state.get("ln")
            if g == 5:
                normalise(ln, 0, b, 1)
            if g == 10:
                ve.wait_ge(pe["wo"], b + 1)
                ln(lambda: ve.tensor_tensor(t1[:, :], ch[0:S, 0:D], bo_r[0][:, :], ALU.add))
                ve.wait_ge(x_res_in, 16 * (b + 1))
                ln.ready()
                ve.tensor_tensor(x1[:, :], x_res[:, :], t1[:, :], ALU.add).then_inc(dv["x1"], 1)
            if g == 11:
                ve.wait_ge(dv["x1"], b + 1)
                norm_stats(ln, x1)
            if g == 12:
                norm_var(ln, "ffn")
            if g == 14:
                norm_apply(x1, "ffn", b).then_inc(dv["y1"], 1)
            if g - 2 in FFN_AT:
                f = FFN_AT.index(g - 2)
                ve.wait_ge(cp[f"ffn{f}"], b + 1)
                ln(lambda: ve.tensor_scalar(ex1[:, :, :], ex[f % 2][:, :, :], 1.0, None, ALU.add))
                ln(lambda: ve.reciprocal(ex1[:, 0, :], ex1[:, 0, :]))
            if g - 3 in FFN_AT:
                f = FFN_AT.index(g - 3)
                ln(lambda: ve.reciprocal(ex1[:, 1, :], ex1[:, 1, :]))
                ln(lambda: ve.tensor_tensor(hg[:, :, :], gu[f % 2][:, :, 0, :], ex1[:, :, :], ALU.mult))
                ln.ready()
                ve.tensor_tensor(hbuf[:, 2 * f:2 * f + 2, :], hg[:, :, :], gu[f % 2][:, :, 1, :], ALU.mult).then_inc(dv[f"h{f}"], 1)
            if g == 29:
                ve.wait_ge(pe["down"], b + 1)
                wait(ve, x2_out, 16 * b)
                ve.tensor_tensor(x2[:, :], x1[:, :], ch[0:S, 0:D], ALU.add).then_inc(dv["x2"], 1)
            if g == 30:
                ve.wait_ge(dv["x2"], b + 1)
                norm_stats(ln, x2)
                norm_var(ln, "q1")
            if g == 32:
                ln(lambda: norm_apply(x2, "q1", b))
            if g in (33, 34, 35):
                quantise(ln, y, dv["q1i"], g - 33)
            if g == 38:
                ve.wait_ge(pe["q1"], b + 1)
                ln(lambda: ve.scalar_tensor_tensor(t1[:, :], ch[0:S, 0:D], s_q[:, 0:1], sw_r[0][:, :], ALU.mult, ALU.mult))
                ln.ready()
                ve.tensor_tensor(q_nat[:, :], t1[:, :], bq_r[1][:, :], ALU.add).then_inc(dv["q1n"], 1)
            if g == 45:
                q_low(1, "q1N", b, dv["q1lo"])
            if g in MASK_AT:
                c = MASK_AT.index(g)
                ve.wait_ge(chk_in, 16 * (b + 1))
                ve.tensor_reduce(mask_abs[:, c:c + 1], mask_chk[:, c * MC:min((c + 1) * MC, T)], AX.X, ALU.max,
                                 apply_absolute_value=True).then_inc(chk_abs, 1)
            if g == 43:
                ve.wait_ge(flag_mm, b + 1)
                ln(lambda: ve.tensor_reduce(mask_any[:, :], kv_bank[0:1, 0:3], AX.X, ALU.max))
                ln.ready()
                ve.tensor_scalar(mask_flag[:, :], mask_any[:, :], 0.0, None, ALU.is_gt).then_inc(flag_ready, 1)
                ln.end()

        L_POST0, L_POST1 = 28, 10

        def slot(main, side, chain, b):
            (ml, mb), (sl, sb_) = main, side
            for g in range(G):
                if exists(sb_) and g - 2 in CHUNK:
                    low(sl, sb_, CHUNK[g - 2])
                for job, units in ((main, UNITS[ml][0]), (side, UNITS[sl][1])):
                    if exists(job[1]):
                        for u in units[g]:
                            reduce_unit(*job, u)
                if exists(mb):
                    if g == FOLD_1:
                        fold(ml, mb, 1)
                    if g == TURN_1 + 1:
                        split(ml, mb, 1)
                if exists(sb_):
                    if g == FOLD_0:
                        fold(sl, sb_, 0)
                    if g == TURN_0 + 1:
                        split(sl, sb_, 0)
                chain(b, g)
                if chain is chain_b and isinstance(b, int) and b == -1 and g >= G // 2:
                    look_up(g - G // 2)
                if chain is chain_a and isinstance(b, int) and b == 0 and g < LOOKUPS - G // 2:
                    look_up(g + G // 2)
                if exists(mb + 1) and g - 1 in SPLITS:
                    c_low(ml, mb + 1, SPLITS[g - 1])

        def slot_a(b):
            slot((0, b), (1, b - 1), chain_a, b)

        def slot_b(b):
            slot((1, b - 1), (0, b + 1), chain_b, b)

        slot_a(-1)
        slot_b(-1)
        for b in range(FIRST):
            slot_a(b)
            slot_b(b)
        with ve.Fori(FIRST, LAST_IT) as b:
            slot_a(b)
            slot_b(b)
        for b in range(LAST_IT, B + 1):
            slot_a(b)
            slot_b(b)
        slot_a(B + 1)

        def over_last(ap, n):
            names = "abc"[:len(ap.shape) - 1]
            left = " ".join(names)
            return ap.rearrange(f"p {left[:-1]}({left[-1]} u) -> p {left} u", u=1).to_broadcast([*ap.shape, n])

        def over_batches(ap):
            return ap.rearrange("p (u e) -> p u e", u=1).to_broadcast([S, B, E])

        ve.wait_ge(x_in, 16)
        with ve.Fori(0, B) as b:
            ve.bn_stats(st6[:, b, :], X[:, b, :]).then_inc(dve_link, 1)
        k[0] += B
        ve.wait_ge(dve_link, k[0])
        m0, m1 = st6[:, :, 1], st6[:, :, 4]
        link(ve.tensor_tensor(mean[:, :], m0, m1, ALU.add))
        link(ve.tensor_scalar(mean[:, :], mean[:, :], 0.5, None, ALU.mult))
        link(ve.tensor_tensor(dif[:, :], m0, m1, ALU.subtract))
        link(ve.scalar_tensor_tensor(dif[:, :], dif[:, :], 0.25, dif[:, :], ALU.mult, ALU.mult))
        link(ve.tensor_tensor(var[:, :], st6[:, :, 2], st6[:, :, 5], ALU.add))
        link(ve.scalar_tensor_tensor(var[:, :], var[:, :], 1.0 / D, dif[:, :], ALU.mult, ALU.add))
        ve.tensor_scalar(var[:, :], var[:, :], EPS_LN, None, ALU.add).then_inc(e["var"], 1)
        link(ve.tensor_tensor(Y[:, :, :], X[:, :, :], over_last(mean[:, :], D), ALU.subtract))
        ve.wait_ge(e["rstd"], 1)
        ve.tensor_tensor(Y[:, :, :], Y[:, :, :], over_last(rst[:, :], D), ALU.mult).then_inc(e["y"], 1)
        link(ve.memset(onesS[:, :], 1.0))
        for i in range(E):
            link(ve.memset(order[:, i:i + 1], float(E - i)))
        ve.wait_ge(e_in, 16 * N_SMALL)
        link(ve.tensor_scalar(nbp2[:, :], bp2_r[:, :], -1.0, None, ALU.mult))
        ve.tensor_copy(wp2b[:, :], wp2[:, 0:1].to_broadcast([128, S])).then_inc(e["small"], 1)
        ve.wait_ge(e["logits"], 1)
        link(ve.tensor_tensor(lg[:, :, :], bank[4][0:S, 0:B * E].rearrange("p (b e) -> p b e", e=E), over_batches(br_r[:, :]), ALU.add))
        link(ve.tensor_reduce(red[:, :], lg[:, :, :], AX.X, ALU.max))
        ve.tensor_tensor(lg[:, :, :], lg[:, :, :], over_last(red[:, :], E), ALU.subtract).then_inc(e["exp_in"], 1)
        ve.wait_ge(e["exp"], 1)
        link(ve.tensor_reduce(red[:, :], pr[:, :, :], AX.X, ALU.add))
        link(ve.reciprocal(red[:, :], red[:, :]))
        link(ve.tensor_tensor(pr[:, :, :], pr[:, :, :], over_last(red[:, :], E), ALU.mult))
        for r in range(TOPK):
            link(ve.tensor_reduce(top[:, r, :], pr[:, :, :], AX.X, ALU.max))
            link(ve.tensor_tensor(eq[:, :, :], pr[:, :, :], over_last(top[:, r, :], E), ALU.is_equal))
            link(ve.tensor_tensor(eq[:, :, :], eq[:, :, :], over_batches(order[:, :]), ALU.mult))
            link(ve.tensor_reduce(red[:, :], eq[:, :, :], AX.X, ALU.max))
            link(ve.tensor_tensor(sel[:, r, :, :], eq[:, :, :], over_last(red[:, :], E), ALU.is_equal))
            link(ve.scalar_tensor_tensor(pr[:, :, :], sel[:, r, :, :], -4.0, pr[:, :, :], ALU.mult, ALU.add))
        ve.tensor_tensor(ew[:, :, :], top[:, :, :], top[:, 0:1, :].to_broadcast([S, TOPK, B]), ALU.subtract).then_inc(e["exp_in"], 1)
        ve.wait_ge(e["exp"], 2)
        link(ve.tensor_reduce(red[:, :], ex3[:, :, :].rearrange("p r b -> p b r"), AX.X, ALU.add))
        link(ve.reciprocal(red[:, :], red[:, :]))
        link(ve.tensor_tensor(ew[:, :, :], ex3[:, :, :], red[:, :].rearrange("p (u b) -> p u b", u=1).to_broadcast([S, TOPK, B]), ALU.mult))
        link(ve.tensor_reduce(cm[:, 1, :, :], sel[:, :, :, :].rearrange("p r b e -> p b e r"), AX.X, ALU.add))
        for r in range(TOPK):
            link(ve.tensor_tensor(sel[:, r, :, :], sel[:, r, :, :], over_last(ew[:, r, :], E), ALU.mult))
        link(ve.tensor_reduce(cm[:, 0, :, :], sel[:, :, :, :].rearrange("p r b e -> p b e r"), AX.X, ALU.add))
        for i in range(2):
            last = ve.tensor_reduce(cms[:, i, :], cm[:, i, :, :].rearrange("p b e -> p e b"), AX.X, ALU.add)
        last.then_inc(e["sums_in"], 1)
        ve.wait_ge(e["sums"], 1)
        link(ve.tensor_scalar(w_e[:, 1, :], bank[5][0:S, E:2 * E], 1.0, None, ALU.max))
        link(ve.reciprocal(w_e[:, 1, :], w_e[:, 1, :]))
        link(ve.tensor_tensor(w_e[:, 0, :], bank[5][0:S, 0:E], w_e[:, 1, :], ALU.mult))
        ve.tensor_tensor(gt[:, :, :], cm[:, 1, :, :].rearrange("p b e -> p e b"), over_last(w_e[:, 0, :], B), ALU.mult).then_inc(e["gates"], 1)
        ve.wait_ge(e["gates"], 1)
        ve.wait_ge(e["init"], B // 2)

        def experts(i):
            for p in range(2):
                n = 2 * i + p
                wait(ve, y_acc, n * B)
                ve.tensor_copy(g_e[p][:, :], gt[:, n, :]).then_inc(ge_ready, 1)
                ve.wait_ge(ge_ready, n + 1)
                for b in range(B):
                    ve.wait_ge(y_mm, n * B + b + 1)
                    ve.scalar_tensor_tensor(acc[:, b, :], bank[4 + b % 4][0:S, 0:D], g_e[p][:, b:b + 1], acc[:, b, :],
                                            ALU.mult, ALU.add).then_inc(y_acc, 1)

        experts(0)
        with ve.Fori(1, E // 2) as i:
            experts(i)
        ve.wait_ge(e["phi"], 3)
        link(ve.tensor_scalar(fac[:, :], fac[:, :], 1.0, None, ALU.add))
        link(ve.reciprocal(fac[:, :], fac[:, :]))
        link(ve.tensor_scalar(fac[:, :], fac[:, :], 0.7, -0.8, ALU.is_gt, ALU.mult))
        link(ve.tensor_scalar(fac[:, :], fac[:, :], 1.0, None, ALU.add))
        ve.wait_ge(y_acc, E * B)
        for b in range(B):
            last = ve.scalar_tensor_tensor(acc[:, b, :], acc[:, b, :], fac[:, b:b + 1], X[:, b, :], ALU.mult, ALU.add)
            if b % 8 == 7:
                last.then_inc(e["final"], 1)


W_AT = (2, 5)
N_DMA = 21
N_CONST = 13
N_SMALL = 7


def kernel(**inputs):
    import concourse.bacc as _bacc
    from concourse.bass_utils import run_bass_kernel_spmd as _run

    x = {k: np.asarray(v) for k, v in inputs.items()}

    def heads_last(w):
        return w.reshape(2, NP, HD, *w.shape[1:]).swapaxes(1, 2).reshape(w.shape)

    host = {
        "x": x["x"], "ctxT": x["ctx_2048"].transpose(0, 2, 1), "mask": x["mask_BxSxS2_ff0"],
        "wqT0": heads_last(x["L0_xattn_Wq"]).T, "woT0": x["L0_xattn_Wo"].T,
        "wq1": heads_last(x["L1_xattn_wq"]), "wo1": x["L1_xattn_wo"],
        "wkT0": heads_last(x["L0_xattn_Wk"]).T, "wkT1": heads_last(x["L1_xattn_wk"]).T,
        "wvT0": x["L0_xattn_Wv"].T, "wvT1": x["L1_xattn_wv"].T,
        "bk0": heads_last(x["L0_xattn_bk"]).reshape(2, 128).T, "bk1": heads_last(x["L1_xattn_bk"]).reshape(2, 128).T,
        "bq0": heads_last(x["L0_xattn_bq"]), "bq1": heads_last(x["L1_xattn_bq"]),
        "bv0": x["L0_xattn_bv"], "bv1": x["L1_xattn_bv"], "bo0": x["L0_xattn_bo"], "bo1": x["L1_xattn_bo"],
        "lut": x["L0_ffn_lut"], "gateT": x["L0_ffn_gate_idx"].T, "upT": x["L0_ffn_up_idx"].T,
        "downT": x["L0_ffn_down_idx"].T,
        "Wr": x["L1_ffn_Wr"], "br": x["L1_ffn_br"], "w1": x["L1_ffn_w1"], "w2": x["L1_ffn_w2"],
        "b1": x["L1_ffn_b1"].reshape(E, HT, 128).transpose(0, 2, 1), "b2": x["L1_ffn_b2"],
        "Wp1": x["L1_ffn_Wp1"], "bp1": x["L1_ffn_bp1"].reshape(128, 1), "Wp2": x["L1_ffn_Wp2"], "bp2": x["L1_ffn_bp2"],
    }
    nc = _bacc.Bacc("TRN2", target_bir_lowering=False, num_devices=1)
    nc.disable_value_cache = True
    arrays, args = {}, {}
    for name, v in host.items():
        v = np.ascontiguousarray(v)
        arrays[f"in_{name}"] = v
        args[name] = nc.dram_tensor(f"in_{name}", v.shape, mybir.dt.from_np(v.dtype), kind="ExternalInput").ap()
    out = nc.dram_tensor("out_0", (B, S, D), F32, kind="ExternalOutput").ap()
    build(nc, args, out)
    r = _run(nc, [arrays], core_ids=[0])
    return r.results[0]["out_0"]
```
